# Optimizing a Trainium2 kernel written in Bass

```python
import numpy as np
import jax
import jax.numpy as jnp

def _softmax(x, axis=-1):
    return jax.nn.softmax(x, axis=axis)

def _gelu(x):
    return jax.nn.gelu(x, approximate=True)

def _silu(x):
    return jax.nn.silu(x)

def _sigmoid(x):
    return jax.nn.sigmoid(x)

def _layernorm(x, axis=-1, eps=1e-05):
    m = jnp.mean(x, axis=axis, keepdims=True)
    v = jnp.var(x, axis=axis, keepdims=True)
    return (x - m) / jnp.sqrt(v + eps)

def _scatter_add(tgt, idx, src, axis=0):
    return tgt.at[idx].add(src)

def _segment_sum(src, seg, n):
    return jax.ops.segment_sum(src, seg, n)
kernel_name = 'mk_gnn_preln_d4_gnn_r8_1fec36'

def setup_inputs(seed: int=0):
    np.random.seed(seed)
    _w = jnp.asarray

    def _rec_inputs():
        import jax
        import jax.numpy as jnp
        _gk = jax.random.key(seed)
        x = -0.0005121 + 1.001 * jax.random.normal(jax.random.fold_in(_gk, 1), (12500, 32), jnp.float32)
        src = jax.random.randint(jax.random.fold_in(_gk, 2), (200000,), 0, 12500, jnp.int32)
        dst = jnp.minimum((12500 * jax.random.uniform(jax.random.fold_in(_gk, 3), (200000,)) ** 2.0).astype(jnp.int32), 99999)
        _o = jnp.argsort(dst, stable=True)
        src = src[_o]
        dst = dst[_o]
        edge_attr_16 = 0.000196303 + 1.00016 * jax.random.normal(jax.random.fold_in(_gk, 12), (200000, 16), jnp.float32)
        return (x, src, dst, edge_attr_16)
    x, src, dst, edge_attr_16 = _rec_inputs()

    def _L0_gnn_setup():
        import jax, jax.numpy as jnp
        import numpy as np
        N = 12500
        E = 200000
        F_IN = 32
        F_OUT = 32
        key = jax.random.key(seed)
        k1, k2, k3, k4, k5 = jax.random.split(key, 5)
        x = jax.random.normal(k1, (N, F_IN), dtype=jnp.float32)
        edge_src = jax.random.randint(k2, (E,), 0, N, dtype=jnp.int32)
        edge_dst = jax.random.randint(k3, (E,), 0, N, dtype=jnp.int32)
        bound = 1.0 / np.sqrt(2 * F_IN)
        W = jax.random.uniform(k4, (2 * F_IN, F_OUT), minval=-bound, maxval=bound, dtype=jnp.float32)
        b = jax.random.uniform(k5, (F_OUT,), minval=-bound, maxval=bound, dtype=jnp.float32)
        return {'x': x, 'W': W, 'b': b, 'edge_src': edge_src, 'edge_dst': edge_dst}
    _L0_gnn_all = _L0_gnn_setup()
    _L0_gnn_in = {k: v for k, v in _L0_gnn_all.items() if k in ('W', 'b')}
    del _L0_gnn_all

    def _L1_gnn_setup():
        import jax, jax.numpy as jnp
        import numpy as np
        N_NODES = 12500
        N_EDGES = 400000
        D_IN = 32
        N_HEADS = 4
        D_HEAD = 8
        key = jax.random.key(seed)
        k1, k2, k3, k4, k5, k6, k7 = jax.random.split(key, 7)
        scale = 1.0 / np.sqrt(D_IN)
        x = jax.random.normal(k1, (N_NODES, D_IN), dtype=jnp.float32)
        Wq = jax.random.normal(k2, (D_IN, N_HEADS * D_HEAD), dtype=jnp.float32) * scale
        Wk = jax.random.normal(k3, (D_IN, N_HEADS * D_HEAD), dtype=jnp.float32) * scale
        Wv = jax.random.normal(k4, (D_IN, N_HEADS * D_HEAD), dtype=jnp.float32) * scale
        Wo = jax.random.normal(k5, (N_HEADS * D_HEAD, D_IN), dtype=jnp.float32) * scale
        src = jax.random.randint(k6, (N_EDGES,), 0, N_NODES)
        dst = jax.random.randint(k7, (N_EDGES,), 0, N_NODES)
        edge_index = jnp.stack([src, dst], axis=0).astype(jnp.int64)
        return {'x': x, 'Wq': Wq, 'Wk': Wk, 'Wv': Wv, 'Wo': Wo, 'edge_index': edge_index}
    _L1_gnn_all = _L1_gnn_setup()
    _L1_gnn_in = {k: v for k, v in _L1_gnn_all.items() if k in ('Wq', 'Wk', 'Wv', 'Wo')}
    del _L1_gnn_all

    def _L2_gnn_setup():
        import jax, jax.numpy as jnp
        import numpy as np
        N_NODES = 6250
        N_EDGES = 200000
        D_NODE = 32
        D_EDGE = 16
        H = 64
        F_OUT = 32
        N_OUT = 32

        def _mlp_params(key, d_in, d_h, d_out):
            k1, k2 = jax.random.split(key)
            s1 = 1.0 / np.sqrt(d_in)
            s2 = 1.0 / np.sqrt(d_h)
            return (jax.random.uniform(k1, (d_in, d_h), jnp.float32, -s1, s1), jnp.zeros((d_h,), jnp.float32), jax.random.uniform(k2, (d_h, d_out), jnp.float32, -s2, s2), jnp.zeros((d_out,), jnp.float32))

        def _mlp(h, W1, b1, W2, b2):
            return jax.nn.relu(jax.nn.relu(h @ W1 + b1) @ W2 + b2)
        key = jax.random.key(seed)
        kx, ke, ka, kf, kb, kn = jax.random.split(key, 6)
        x = jax.random.normal(kx, (N_NODES, D_NODE), jnp.float32)
        edge_index = jax.random.randint(ke, (2, N_EDGES), 0, N_NODES, jnp.int64)
        edge_attr = jax.random.normal(ka, (N_EDGES, D_EDGE), jnp.float32)
        d_flow_in = 2 * D_NODE + D_EDGE
        W1f, b1f, W2f, b2f = _mlp_params(kf, d_flow_in, H, F_OUT)
        W1b, b1b, W2b, b2b = _mlp_params(kb, d_flow_in, H, F_OUT)
        W1n, b1n, W2n, b2n = _mlp_params(kn, 2 * F_OUT, H, N_OUT)
        return dict(x=x, edge_index=edge_index, edge_attr=edge_attr, W1f=W1f, b1f=b1f, W2f=W2f, b2f=b2f, W1b=W1b, b1b=b1b, W2b=W2b, b2b=b2b, W1n=W1n, b1n=b1n, W2n=W2n, b2n=b2n)
    _L2_gnn_all = _L2_gnn_setup()
    _L2_gnn_in = {k: v for k, v in _L2_gnn_all.items() if k in ('W1f', 'b1f', 'W2f', 'b2f', 'W1b', 'b1b', 'W2b', 'b2b', 'W1n', 'b1n', 'W2n', 'b2n')}
    del _L2_gnn_all

    def _L3_gnn_setup():
        import jax, jax.numpy as jnp
        import numpy as np
        N_NODES = 6250
        DEG = 16
        N_HEAD = 4
        F_IN = 32
        F_OUT = 32
        key = jax.random.key(seed)
        k_h, k_w, k_fw, k_fb = jax.random.split(key, 4)
        h = jax.random.normal(k_h, (N_NODES, F_IN), dtype=jnp.float32)
        src = jnp.repeat(jnp.arange(N_NODES, dtype=jnp.int64), DEG)
        offs = (jnp.arange(DEG, dtype=jnp.int64) + 1) * 97
        dst = (src.reshape(N_NODES, DEG) + offs[None, :]).reshape(-1) % N_NODES
        edge_index = jnp.stack([src, dst], axis=0)
        gain = 1.414
        bound_w = gain * np.sqrt(6.0 / (F_IN + F_OUT))
        w = jax.random.uniform(k_w, (N_HEAD, F_IN, F_OUT), jnp.float32, -bound_w, bound_w)
        bound_fc = np.sqrt(1.0 / (2 * F_OUT))
        fc_w = jax.random.uniform(k_fw, (1, 2 * F_OUT), jnp.float32, -bound_fc, bound_fc)
        fc_b = jax.random.uniform(k_fb, (1,), jnp.float32, -bound_fc, bound_fc)
        bias = jnp.zeros((F_OUT,), jnp.float32)
        return {'h': h, 'edge_index': edge_index, 'w': w, 'fc_w': fc_w, 'fc_b': fc_b, 'bias': bias}
    _L3_gnn_all = _L3_gnn_setup()
    _L3_gnn_in = {k: v for k, v in _L3_gnn_all.items() if k in ('w', 'fc_w', 'fc_b', 'bias')}
    del _L3_gnn_all
    return {'x': x, 'src': src, 'dst': dst, 'edge_attr_16': edge_attr_16, 'L0_gnn_W': _L0_gnn_in['W'], 'L0_gnn_b': _L0_gnn_in['b'], 'L1_gnn_Wq': _L1_gnn_in['Wq'], 'L1_gnn_Wk': _L1_gnn_in['Wk'], 'L1_gnn_Wv': _L1_gnn_in['Wv'], 'L1_gnn_Wo': _L1_gnn_in['Wo'], 'L2_gnn_W1f': _L2_gnn_in['W1f'], 'L2_gnn_b1f': _L2_gnn_in['b1f'], 'L2_gnn_W2f': _L2_gnn_in['W2f'], 'L2_gnn_b2f': _L2_gnn_in['b2f'], 'L2_gnn_W1b': _L2_gnn_in['W1b'], 'L2_gnn_b1b': _L2_gnn_in['b1b'], 'L2_gnn_W2b': _L2_gnn_in['W2b'], 'L2_gnn_b2b': _L2_gnn_in['b2b'], 'L2_gnn_W1n': _L2_gnn_in['W1n'], 'L2_gnn_b1n': _L2_gnn_in['b1n'], 'L2_gnn_W2n': _L2_gnn_in['W2n'], 'L2_gnn_b2n': _L2_gnn_in['b2n'], 'L3_gnn_w': _L3_gnn_in['w'], 'L3_gnn_fc_w': _L3_gnn_in['fc_w'], 'L3_gnn_fc_b': _L3_gnn_in['fc_b'], 'L3_gnn_bias': _L3_gnn_in['bias']}

def reference(x, src, dst, edge_attr_16, L0_gnn_W, L0_gnn_b, L1_gnn_Wq, L1_gnn_Wk, L1_gnn_Wv, L1_gnn_Wo, L2_gnn_W1f, L2_gnn_b1f, L2_gnn_W2f, L2_gnn_b2f, L2_gnn_W1b, L2_gnn_b1b, L2_gnn_W2b, L2_gnn_b2b, L2_gnn_W1n, L2_gnn_b1n, L2_gnn_W2n, L2_gnn_b2n, L3_gnn_w, L3_gnn_fc_w, L3_gnn_fc_b, L3_gnn_bias):
    import jax
    import jax.numpy as jnp

    def _L0_gnn_ref(x, W, b, edge_src, edge_dst):
        import jax, jax.numpy as jnp
        import numpy as np
        N = 12500
        E = 200000
        F_IN = 32
        F_OUT = 32
        n = x.shape[0]
        msgs = x[edge_src]
        summed = jax.ops.segment_sum(msgs, edge_dst, num_segments=n)
        cnt = jax.ops.segment_sum(jnp.ones_like(edge_dst, dtype=x.dtype), edge_dst, num_segments=n)
        neigh_mean = summed / jnp.maximum(cnt, 1.0)[:, None]
        h = jnp.concatenate([x, neigh_mean], axis=1)
        return jax.nn.relu(h @ W + b)

    def _L1_gnn_ref(x, Wq, Wk, Wv, Wo, edge_index):
        import jax, jax.numpy as jnp
        import numpy as np
        N_NODES = 12500
        N_EDGES = 400000
        D_IN = 32
        N_HEADS = 4
        D_HEAD = 8
        N = x.shape[0]
        src, dst = (edge_index[0], edge_index[1])
        q = (x @ Wq).reshape(N, N_HEADS, D_HEAD)
        k = (x @ Wk).reshape(N, N_HEADS, D_HEAD)
        v = (x @ Wv).reshape(N, N_HEADS, D_HEAD)
        inv_sqrt_d = jnp.asarray(1.0 / np.sqrt(D_HEAD), dtype=x.dtype)
        scores = jnp.einsum('ehd,ehd->eh', q[dst], k[src]) * inv_sqrt_d
        m = jax.ops.segment_max(scores, dst, num_segments=N)
        m = jnp.where(jnp.isfinite(m), m, jnp.zeros_like(m))
        e = jnp.exp(scores - m[dst])
        denom = jax.ops.segment_sum(e, dst, num_segments=N)
        msg = jax.ops.segment_sum(e[:, :, None] * v[src], dst, num_segments=N)
        attn_out = msg / jnp.maximum(denom, 1e-16)[:, :, None]
        out = attn_out.reshape(N, N_HEADS * D_HEAD) @ Wo
        return x + out

    def _L2_gnn_ref(x, edge_index, edge_attr, W1f, b1f, W2f, b2f, W1b, b1b, W2b, b2b, W1n, b1n, W2n, b2n):
        import jax, jax.numpy as jnp
        import numpy as np
        N_NODES = 6250
        N_EDGES = 200000
        D_NODE = 32
        D_EDGE = 16
        H = 64
        F_OUT = 32
        N_OUT = 32

        def _mlp_params(key, d_in, d_h, d_out):
            k1, k2 = jax.random.split(key)
            s1 = 1.0 / np.sqrt(d_in)
            s2 = 1.0 / np.sqrt(d_h)
            return (jax.random.uniform(k1, (d_in, d_h), jnp.float32, -s1, s1), jnp.zeros((d_h,), jnp.float32), jax.random.uniform(k2, (d_h, d_out), jnp.float32, -s2, s2), jnp.zeros((d_out,), jnp.float32))

        def _mlp(h, W1, b1, W2, b2):
            return jax.nn.relu(jax.nn.relu(h @ W1 + b1) @ W2 + b2)
        past, future = (edge_index[0], edge_index[1])
        x_past = x[past]
        x_future = x[future]
        fwd_in = jnp.concatenate([x_future, x_past, edge_attr], axis=1)
        flow_fwd = _mlp(fwd_in, W1f, b1f, W2f, b2f)
        fwd_agg = jax.ops.segment_sum(flow_fwd, future, num_segments=x.shape[0])
        bwd_in = jnp.concatenate([x_past, x_future, edge_attr], axis=1)
        flow_bwd = _mlp(bwd_in, W1b, b1b, W2b, b2b)
        bwd_agg = jax.ops.segment_sum(flow_bwd, past, num_segments=x.shape[0])
        flow_total = jnp.concatenate([fwd_agg, bwd_agg], axis=1)
        return _mlp(flow_total, W1n, b1n, W2n, b2n)

    def _L3_gnn_ref(h, edge_index, w, fc_w, fc_b, bias):
        import jax, jax.numpy as jnp
        import numpy as np
        N_NODES = 6250
        DEG = 16
        N_HEAD = 4
        F_IN = 32
        F_OUT = 32
        n_head, f_in, f_out = w.shape
        n = h.shape[0]
        src, dst = (edge_index[0], edge_index[1])
        hp = jnp.einsum('nf,hfo->hno', h, w)
        w_src = fc_w[0, :f_out]
        w_dst = fc_w[0, f_out:]
        a_src = jnp.einsum('hnf,f->hn', hp, w_src)
        a_dst = jnp.einsum('hnf,f->hn', hp, w_dst)
        e = a_src[:, src] + a_dst[:, dst] + fc_b[0]
        e = jax.nn.leaky_relu(e, negative_slope=0.2)
        seg_max = jax.ops.segment_max(e.T, src, num_segments=n)
        e = jnp.exp(e - seg_max.T[:, src])
        seg_sum = jax.ops.segment_sum(e.T, src, num_segments=n)
        att = e / seg_sum.T[:, src]
        msg = att[:, :, None] * hp[:, dst, :]
        agg = jax.vmap(lambda m: jax.ops.segment_sum(m, src, num_segments=n))(msg)
        out = agg.mean(axis=0) + bias
        return out
    edge_index = jnp.stack([src, dst])
    h = jnp.maximum(_layernorm(x, axis=-1), 0.0)
    x = x + _L0_gnn_ref(h, L0_gnn_W, L0_gnn_b, src, dst)
    h = jnp.maximum(_layernorm(x, axis=-1), 0.0)
    x = x + _L1_gnn_ref(h, L1_gnn_Wq, L1_gnn_Wk, L1_gnn_Wv, L1_gnn_Wo, edge_index)
    h = jnp.maximum(_layernorm(x, axis=-1), 0.0)
    x = x + _L2_gnn_ref(h, edge_index, edge_attr_16, L2_gnn_W1f, L2_gnn_b1f, L2_gnn_W2f, L2_gnn_b2f, L2_gnn_W1b, L2_gnn_b1b, L2_gnn_W2b, L2_gnn_b2b, L2_gnn_W1n, L2_gnn_b1n, L2_gnn_W2n, L2_gnn_b2n)
    h = jnp.maximum(_layernorm(x, axis=-1), 0.0)
    x = x + _L3_gnn_ref(h, edge_index, L3_gnn_w, L3_gnn_fc_w, L3_gnn_fc_b, L3_gnn_bias)
    return x

_drawn_inputs = setup_inputs


def setup_inputs(seed=0):
    import zlib

    import numpy as np

    out = dict(_drawn_inputs(seed))
    spreads = {'L2_gnn_b1f': (0.0, 0.1),
     'L2_gnn_b2f': (0.0, 0.1),
     'L2_gnn_b1b': (0.0, 0.1),
     'L2_gnn_b2b': (0.0, 0.1),
     'L2_gnn_b1n': (0.0, 0.763),
     'L2_gnn_b2n': (0.0, 0.1),
     'L3_gnn_bias': (0.0, 0.1)}
    factors = {}
    for name, (base, spread) in spreads.items():
        noise = np.random.default_rng([zlib.crc32(name.encode()), seed]).standard_normal(out[name].shape)
        drawn = base * np.exp(spread * noise) if base else spread * noise
        out[name] = jnp.asarray(drawn.astype(out[name].dtype))
    for name, factor in factors.items():
        out[name] = (out[name] * factor).astype(out[name].dtype)
    return out
```

```python
import concourse.bass as bass
from concourse import mybir
from contextlib import ExitStack

F32 = mybir.dt.float32
BF16 = mybir.dt.bfloat16
I32 = mybir.dt.int32
ALU = mybir.AluOpType
ACT = mybir.ActivationFunctionType
X = mybir.AxisListType.X
ds = bass.ds

N, E, D, DE = 12500, 200000, 32, 16
P = 128
NB = (N + P - 1) // P
FULL = N // P
NBP = (NB + 7) // 8 * 8
NP = NBP * P
HEADS, DH, H2 = 4, 8, 64
EP = 125
EC = E // EP
CB = 5
T = 4
GE = T * P
U = 4
NG = ((E - NB) // GE + NB + U - 1) // U * U
GP = max(d for d in range(1, P + 1) if NG % d == 0)
GQ = NG // GP
S = NG * GE
RW = 2 + DE
NT = NG * T
TR = max(d for d in range(1, P + 1) if NT % d == 0)
CG = max(d for d in range(1, 65) if NG % d == 0)
BIG = float(2 ** 20)
NONE = -2.0 * BIG
FAR = 1000.0


class At:

    def __init__(self, g, slot, turn):
        self.g, self.slot, self.turn = g, slot, turn
        self.first = isinstance(turn, int) and turn == 0


def group_steps(eng, groups, depth, lag):
    for t in range(depth):
        yield lambda k, t=t: At(t - k, (t - k) % depth, 0) if t >= k else None
    with eng.Fori(1, groups // depth) as i:
        for u in range(depth):
            yield lambda k, u=u: At(i * depth + (u - k), (u - k) % depth, i + (u - k) // depth)
    for t in range(groups, groups + lag):
        yield lambda k, t=t: At(t - k, (t - k) % depth, (t - k) // depth) if t - k < groups else None


def gnn_kernel(nc, x, src, dst, edge_attr, W0, b0, Wq, Wk, Wv, Wo, W1f, b1f, W2f, b2f, W1b, b1b, W2b, b2b,
               W1n, b1n, W2n, b2n, w3, fc_w, fc_b, bias3, out):
    ctx = ExitStack()
    with ctx:
        used = {}

        def unique(name):
            used[name] = used.get(name, 0) + 1
            return name if used[name] == 1 else f"{name}_{used[name]}"

        class Scope(ExitStack):
            sems = None

            def __exit__(self, *error):
                if self.sems and error[0] is None:
                    with nc.Block() as block:
                        @block.gpsimd
                        def _(pool):
                            for s in self.sems:
                                pool.sem_clear(s)
                return super().__exit__(*error)

        def sb(name, shape, dt, c=ctx):
            return c.enter_context(nc.sbuf_tensor(unique(name), shape, dt))

        def sem(name, c=ctx):
            s = c.enter_context(nc.semaphore(unique(name)))
            c.sems = (c.sems or []) + [s]
            return s

        def dram(name, shape, dt):
            return nc.dram_tensor(name, shape, dt).ap()

        low = ctx.enter_context(nc.psum_tensor("low", [P, 2, 512], F32))
        wide = ctx.enter_context(nc.psum_tensor("wide", [P, 4, 512], F32))
        high = ctx.enter_context(nc.psum_tensor("high", [P, 2, 512], F32))
        psum = [t[:, i, :] for t, n in ((low, 2), (wide, 4), (high, 2)) for i in range(n)]

        pool_dma = [ctx.enter_context(nc.semaphore(f"pool_dma{u}")) for u in range(8)]
        pool_base = [0] * 8

        rec = [dram(f"rec{k}", [S, RW], I32) for k in range(2)]
        rowT = [dram(f"rowT{k}", [NT, P], BF16) for k in range(2)]
        blk_d = [dram(f"blk{k}", [1, NG], I32) for k in range(2)]
        gath = [dram(f"gath{i}", [NP, w], F32) for i, w in enumerate((D, 2 * D, D, D + HEADS))]
        locl = [None, dram("locl1", [NP, 3 * D], BF16), dram("locl2f", [NP, 3 * H2], BF16),
                dram("locl3", [NP, 3 * HEADS], BF16), dram("locl2b", [NP, 3 * H2], BF16)]

        Xs = sb("Xs", [P, NBP, D], F32)
        Hs = sb("Hs", [P, NBP, D], F32)
        idx = [sb(f"idx{k}", [P, NT], I32) for k in range(2)]
        near = [sb(f"near{k}", [P, NT], F32) for k in range(2)]
        blk = [sb(f"blkrow{k}", [1, NG], I32) for k in range(2)]
        iof = sb("iof", [P, P], F32)
        iob = sb("iob", [P, P], BF16)
        iop = sb("iop", [P, 1], F32)
        ident = sb("ident", [P, P], F32)
        bigI = sb("bigI", [P, P], BF16)
        onesb = sb("onesb", [P, P], BF16)
        onesf = sb("onesf", [1, P], F32)
        tri = sb("tri", [P, P], BF16)
        sel = sb("sel", [HEADS, HEADS, P], BF16)
        eps = sb("eps", [P, 1], F32)

        def chained(eng, name, c):
            s, n = sem(name, c), [0]

            def link(ins):
                n[0] += 1
                ins.then_inc(s, 1)
                eng.wait_ge(s, n[0])
            return link

        with Scope() as c:
            ioi = sb("ioi", [P, P], I32, c)
            iopi = sb("iopi", [P, 1], I32, c)
            empty = sb("empty", [P, CG * RW], I32, c)
            s_io, s_x0, s_x, s_e, s_rec = (sem(n, c) for n in ("s_io", "s_x0", "s_x", "s_e", "s_rec"))
            s_c = sem("s_c", c)
            with nc.Block() as block:
                @block.gpsimd
                def _(pool):
                    pool.iota(ioi[:, :], pattern=[[1, P]], base=0, channel_multiplier=0).then_inc(s_io, 1)
                    pool.iota(iopi[:, :], pattern=[[0, 1]], base=0, channel_multiplier=1).then_inc(s_io, 1)

                @block.vector
                def _(dve):
                    link = chained(dve, "chain_c", c)
                    link(dve.memset(empty[:, :], 0))
                    ids = empty[:, :].rearrange("p (s w) -> p s w", w=RW)[:, :, 0:2]
                    dve.memset(ids, -1).then_inc(s_e, 1)
                    dve.memset(Xs[:, :, :], 0.0).then_inc(s_x0, 1)
                    dve.memset(onesb[:, :], 1.0)
                    dve.memset(onesf[:, :], 1.0)
                    dve.memset(eps[:, :], 1e-5)
                    dve.wait_ge(s_io, 2)
                    dve.tensor_copy(iof[:, :], ioi[:, :])
                    dve.tensor_copy(iob[:, :], ioi[:, :])
                    link(dve.tensor_copy(iop[:, :], iopi[:, :]))
                    dve.tensor_scalar(ident[:, :], iof[:, :], iop[:, 0:1], None, ALU.is_equal)
                    dve.tensor_scalar(bigI[:, :], iof[:, :], iop[:, 0:1], BIG, ALU.is_equal, ALU.mult)
                    dve.tensor_scalar(tri[:, :], iof[:, :], iop[:, 0:1], None, ALU.is_gt)
                    link(dve.tensor_scalar(sel[:, :, :], iof[0:HEADS, 0:HEADS].unsqueeze(2).to_broadcast([HEADS, HEADS, P]),
                                           iop[0:HEADS, 0:1], None, ALU.is_equal))

                @block.sync
                def _(sp):
                    sp.wait_ge(s_x0, 1)
                    sp.dma_start(Xs[:, 0:FULL, :], x[0:FULL * P, :].rearrange("(b p) f -> p b f", p=P)).then_inc(s_x, 16)
                    sp.dma_start(Xs[0:N - FULL * P, FULL, :], x[FULL * P:N, :]).then_inc(s_x, 16)
                    sp.wait_ge(s_e, 1)
                    for k in range(2):
                        view = rec[k].rearrange("(p a s) w -> a p (s w)", p=P, s=CG)
                        for a in range(S // P // CG):
                            sp.dma_start(view[a], empty[:, :]).then_inc(s_rec, 16)
                    sp.wait_ge(s_x, 32)
                    sp.wait_ge(s_rec, 2 * (S // P // CG) * 16)

        with Scope() as c:
            ids = [sb(f"ids{k}", [EP, EC], I32, c) for k in range(2)]
            hi32 = sb("hi32", [EP, EC], I32, c)
            hi = [sb(f"hi{k}", [EP, EC], BF16, c) for k in range(2)]
            ohz = [[sb(f"oh{k}{u}", [P, 2 * CB - 1, NB], BF16, c) for u in range(U)] for k in range(2)]
            oh = [[t[:, CB - 1:, :] for t in ts] for ts in ohz]
            cnt = sb("cnt", [P, NB], F32, c)
            cnti = sb("cnti", [P, NB], I32, c)
            padded = sb("padded", [P, NB], F32, c)
            ends = sb("ends", [P, NB], F32, c)
            ones98 = sb("ones98", [P, NB], F32, c)
            gi = sb("gi", [GP, GQ], I32, c)
            gf = sb("gf", [GP, GQ], F32, c)
            past = sb("past", [GP, GQ, NB], F32, c)
            gb = sb("gb", [GP, GQ], F32, c)
            gbi = [sb(f"gbi{k}", [GP, GQ], I32, c) for k in range(2)]
            run = [sb(f"run{k}", [P, NB], F32, c) for k in range(2)]
            recs = [sb(f"recs{u}", [EP, CB, RW], I32, c) for u in range(U)]
            val = [sb(f"val{k}", [EP, CB, NB], F32, c) for k in range(2)]
            pos = [sb(f"pos{k}", [EP, CB], F32, c) for k in range(2)]
            posi = [[sb(f"posi{k}{u}", [EP, CB], I32, c) for u in range(U)] for k in range(2)]
            s_ids, s_hi, s_oh, s_hist, s_histd = (sem(n, c) for n in ("s_ids", "s_hi", "s_oh", "s_hist", "s_histd"))
            s_gi, s_gbi, s_blk, s_start = (sem(n, c) for n in ("s_gi", "s_gbi", "s_blk", "s_start"))
            NC = EC // CB

            with nc.Block() as block:
                @block.sync
                def _(sp):
                    for k, a in enumerate((dst, src)):
                        sp.dma_start(ids[k][:, :], a.rearrange("(p c) -> p c", p=EP)).then_inc(s_ids, 16)
                    sp.wait_ge(s_gbi, 2)
                    for k in range(2):
                        sp.dma_start(blk_d[k].rearrange("a (p q) -> (a p) q", p=GP), gbi[k][:, :]).then_inc(s_blk, 16)
                    sp.wait_ge(s_blk, 32)
                    for k in range(2):
                        sp.dma_start(blk[k][:, :], blk_d[k]).then_inc(s_blk, 16)
                    sp.wait_ge(s_blk, 64)

                @block.gpsimd
                def _(pool):
                    pool.iota(gi[:, :], pattern=[[1, GQ]], base=0, channel_multiplier=GQ).then_inc(s_gi, 1)

                @block.vector
                def _(dve):
                    link = chained(dve, "chain_h", c)
                    for k in range(2):
                        for u in range(U):
                            dve.memset(ohz[k][u][:, 0:CB - 1, :], 0.0)
                    dve.wait_ge(s_ids, 32)
                    for k in range(2):
                        link(dve.tensor_scalar(hi32[:, :], ids[k][:, :], 7, None, ALU.arith_shift_right))
                        link(dve.tensor_copy(hi[k][:, :], hi32[:, :]))
                    for step in group_steps(dve, NC, 2, 0):
                        at = step(0)
                        if not at.first:
                            dve.wait_ge(s_hist, at.g - 1)
                        for k in range(2):
                            ins = dve.tensor_tensor(oh[k][at.slot][0:EP, :, :],
                                                    hi[k][:, ds(at.g * CB, CB)].unsqueeze(2).to_broadcast([EP, CB, NB]),
                                                    iob[0:EP, 0:NB].unsqueeze(1).to_broadcast([EP, CB, NB]), ALU.is_equal)
                        ins.then_inc(s_oh, 1)
                    dve.wait_ge(s_histd, 1)
                    dve.wait_ge(s_gi, 1)
                    link(dve.tensor_copy(gf[:, :], gi[:, :]))
                    link(dve.memset(ones98[:, :], 1.0))
                    for k in range(2):
                        link(dve.tensor_reduce(cnt[:, :], psum[k][:, 0:CB * NB].rearrange("p (c b) -> p b c", c=CB), X, ALU.add))
                        link(dve.tensor_scalar(cnti[:, :], cnt[:, :], float(GE - 1), None, ALU.add))
                        link(dve.tensor_scalar(cnti[:, :], cnti[:, :], -GE, None, ALU.bitwise_and))
                        link(dve.tensor_copy(padded[:, :], cnti[:, :]))
                        link(dve.tensor_tensor_scan(ends[:, :], ones98[:, :], padded[:, :], 0.0, ALU.mult, ALU.add))
                        link(dve.tensor_tensor(run[k][:, :], ends[:, :], padded[:, :], ALU.subtract))
                        link(dve.tensor_scalar(ends[:, :], ends[:, :], 1.0 / GE, None, ALU.mult))
                        link(dve.tensor_tensor(past[:, :, :], gf[:, :].unsqueeze(2).to_broadcast([GP, GQ, NB]),
                                               ends[0:GP, :].unsqueeze(1).to_broadcast([GP, GQ, NB]), ALU.is_ge))
                        link(dve.tensor_reduce(gb[:, :], past[:, :, :], X, ALU.add))
                        dve.tensor_scalar(gbi[k][:, :], gb[:, :], float(NB - 1), None, ALU.min).then_inc(s_gbi, 1)

                @block.tensor
                def _(pe):
                    for step in group_steps(pe, NC, 2, 0):
                        at = step(0)
                        pe.wait_ge(s_oh, at.g + 1)
                        for k in range(2):
                            ins = pe.matmul(psum[k][:, 0:CB * NB], onesb[0:EP, :],
                                            oh[k][at.slot][0:EP, :, :].rearrange("p c b -> p (c b)"),
                                            start=at.first and at.slot == 0, stop=False, skip_group_check=True)
                        ins.then_inc(s_hist, 1)
                    pe.wait_ge(s_hist, NC)
                    pe.nop().then_inc(s_histd, 1)

            s_oh2, s_rk, s_val, s_pos, s_ids2, s_nxt = (sem(n, c) for n in ("s_oh2", "s_rk", "s_val", "s_pos", "s_ids2", "s_nxt"))
            s_ea = [sem(f"s_ea{u}", c) for u in range(U)]
            s_sc = pool_dma
            ea_v = edge_attr.bitcast(I32).rearrange("(p c) f -> p c f", p=EP)

            with nc.Block() as block:
                @block.sync
                def _(sp):
                    for step in group_steps(sp, NC, U, 0):
                        at = step(0)
                        if not at.first:
                            sp.wait_ge(s_sc[at.slot], at.turn * (16 * 2 * CB))
                        sp.dma_start(recs[at.slot][:, :, 2:RW], ea_v[:, ds(at.g * CB, CB), :]).then_inc(s_ea[at.slot], 16)

                @block.gpsimd
                def _(pool):
                    for step in group_steps(pool, NC, U, 0):
                        at = step(0)
                        pool.wait_ge(s_ea[at.slot], (at.turn + 1) * 16)
                        pool.wait_ge(s_pos, at.g + 1)
                        pool.sem_inc(s_start, 1)
                        for k in range(2):
                            for j in range(CB):
                                pool.indirect_dma_start(rec[k], bass.IndirectOffsetOnAxis(ap=posi[k][at.slot][:, j:j + 1], axis=0),
                                                        recs[at.slot][:, j, :], None).then_inc(s_sc[at.slot], 16)
                    for u in range(U):
                        pool.wait_ge(s_sc[u], NC // U * 16 * 2 * CB)
                        pool_base[u] = NC // U * 16 * 2 * CB

                @block.tensor
                def _(pe):
                    for step in group_steps(pe, NC, U, 0):
                        at = step(0)
                        pe.wait_ge(s_oh2, at.g + 1)
                        if not (at.first and at.slot < 2):
                            pe.wait_ge(s_pos, at.g - 1)
                        for k in range(2):
                            o = oh[k][at.slot]
                            for j in range(CB):
                                pe.matmul(psum[2 * k + at.slot % 2][:, 0:CB * NB], (onesb if j else tri)[0:EP, 0:P],
                                          ohz[k][at.slot][0:EP, CB - 1 - j:2 * CB - 1 - j, :].rearrange("p c b -> p (c b)"),
                                          start=j == 0, stop=j == CB - 1)
                            for j in range(CB):
                                ins = pe.matmul(psum[4 + 2 * k + at.slot % 2][:, 0:NB], onesb[0:EP, 0:P], o[0:EP, j, :],
                                                start=j == 0, stop=j == CB - 1)
                        ins.then_inc(s_rk, 1)

                @block.vector
                def _(dve):
                    for step in group_steps(dve, NC, U, 1):
                        at = step(0)
                        if at:
                            if not at.first:
                                dve.wait_ge(s_sc[at.slot], at.turn * (16 * 2 * CB))
                            for k in range(2):
                                dve.tensor_tensor(oh[k][at.slot][0:EP, :, :],
                                                  hi[k][:, ds(at.g * CB, CB)].unsqueeze(2).to_broadcast([EP, CB, NB]),
                                                  iob[0:EP, 0:NB].unsqueeze(1).to_broadcast([EP, CB, NB]),
                                                  ALU.is_equal).then_inc(s_oh2 if k else s_ids2, 1)
                            ri = recs[at.slot]
                            for k in range(2):
                                ins = dve.tensor_copy(ri[:, :, 1 - k:2 - k], ids[k][:, ds(at.g * CB, CB)].unsqueeze(2))
                        at = step(1)
                        if at:
                            dve.wait_ge(s_rk, at.g + 1)
                            dve.wait_ge(s_oh2, at.g + 1)
                            if not (isinstance(at.g, int) and at.g == 0):
                                dve.wait_ge(s_nxt, at.g * 2)
                            for k in range(2):
                                dve.tensor_tensor(val[k][:, :, :], psum[2 * k + at.slot % 2][0:EP, 0:CB * NB].rearrange("p (c b) -> p c b", c=CB),
                                                  run[k][0:EP, :].unsqueeze(1).to_broadcast([EP, CB, NB]), ALU.add).then_inc(s_val, 1)
                            for k in range(2):
                                dve.wait_ge(s_val, at.g * 6 + 1 + k)
                                dve.tensor_tensor(val[k][:, :, :], val[k][:, :, :], oh[k][at.slot][0:EP, :, :], ALU.mult).then_inc(s_val, 1)
                            for k in range(2):
                                dve.tensor_tensor(run[k][:, :], run[k][:, :], psum[4 + 2 * k + at.slot % 2][:, 0:NB], ALU.add).then_inc(s_nxt, 1)
                            for k in range(2):
                                dve.wait_ge(s_val, at.g * 6 + 3 + k)
                                dve.tensor_reduce(pos[k][:, :], val[k][:, :, :], X, ALU.add).then_inc(s_val, 1)
                            for k in range(2):
                                dve.wait_ge(s_val, at.g * 6 + 5 + k)
                                ins = dve.tensor_copy(posi[k][at.slot][:, :], pos[k][:, :])
                            ins.then_inc(s_pos, 1)


        with Scope() as c:
            back = [sb(f"back{u}", [P, CG, T, RW], I32, c) for u in range(2)]
            low7 = sb("low7", [P, CG, T], I32, c)
            none = sb("none", [P, CG, T], F32, c)
            rows = [sb(f"rows{k}", [TR, NT // TR, P], BF16, c) for k in range(2)]
            s_back = [sem(f"s_back{u}", c) for u in range(2)]
            s_free, s_near, s_rt, s_rows, s_rowd = (sem(n, c) for n in ("s_free", "s_near", "s_rt", "s_rows", "s_rowd"))
            CH = NG // CG
            with nc.Block() as block:
                @block.sync
                def _(sp):
                    for n in range(2 * CH):
                        k, a = divmod(n, CH)
                        if n >= 2:
                            sp.wait_ge(s_free, n - 1)
                        sp.dma_start(back[n % 2].rearrange("p g j w -> p g (j w)"),
                                     rec[k].rearrange("(g p j) w -> p g (j w)", p=P, j=T)[:, a * CG:(a + 1) * CG, :])\
                          .then_inc(s_back[n % 2], 16)
                    for k in range(2):
                        sp.wait_ge(s_rows, (k + 1) * (NT // TR))
                        sp.dma_start(rowT[k].rearrange("(b r) p -> r b p", r=TR), rows[k][:, :, :]).then_inc(s_rowd, 16)
                    sp.wait_ge(s_rowd, 32)

                @block.vector
                def _(dve):
                    link = chained(dve, "chain_b", c)
                    for n in range(2 * CH):
                        k, a = divmod(n, CH)
                        dve.wait_ge(s_back[n % 2], (n // 2 + 1) * 16)
                        if n:
                            dve.wait_ge(s_free, n)
                        far, nr = back[n % 2][:, :, :, k], back[n % 2][:, :, :, 1 - k]
                        at = slice(a * CG * T, (a + 1) * CG * T)
                        dve.tensor_scalar(idx[k][:, at].rearrange("p (g j) -> p g j", j=T), far, 0.0, None, ALU.max)
                        dve.tensor_scalar(none[:, :, :], nr, 0.0, FAR, ALU.is_lt, ALU.mult)
                        link(dve.tensor_scalar(low7[:, :, :], nr, P - 1, None, ALU.bitwise_and))
                        dve.tensor_tensor(near[k][:, at].rearrange("p (g j) -> p g j", j=T), low7[:, :, :], none[:, :, :], ALU.add)\
                           .then_inc(s_free, 1)

                @block.tensor
                def _(pe):
                    for k in range(2):
                        pe.wait_ge(s_free, (k + 1) * CH)
                        for n in range(NT // TR):
                            m = k * (NT // TR) + n
                            if m >= 8:
                                pe.wait_ge(s_rows, m - 7)
                            pe.transpose(psum[m % 8][0:TR, 0:P], near[k][:, n * TR:(n + 1) * TR], ident[:, :]).then_inc(s_rt, 1)

                @block.scalar
                def _(act):
                    for k in range(2):
                        for n in range(NT // TR):
                            m = k * (NT // TR) + n
                            act.wait_ge(s_rt, m + 1)
                            act.activation(rows[k][:, n, :], psum[m % 8][0:TR, 0:P], ACT.Copy).then_inc(s_rows, 1)

        def normalise(c):
            mean = sb("mean", [P, NBP], F32, c)
            var = sb("var", [P, NBP], F32, c)
            dev = sb("dev", [P, NBP], F32, c)
            sq = sb("sq", [P, NBP, D], F32, c)
            s_var, s_sd = sem("s_var", c), sem("s_sd", c)
            wide3 = [P, NBP, D]
            with nc.Block() as block:
                @block.vector
                def _(dve):
                    link = chained(dve, "chain_n", c)
                    link(dve.tensor_reduce(mean[:, :], Xs[:, :, :], X, ALU.add))
                    link(dve.tensor_scalar(mean[:, :], mean[:, :], 1.0 / D, None, ALU.mult))
                    link(dve.tensor_tensor(Hs[:, :, :], Xs[:, :, :], mean[:, :].unsqueeze(2).to_broadcast(wide3), ALU.subtract))
                    link(dve.tensor_tensor(sq[:, :, :], Hs[:, :, :], Hs[:, :, :], ALU.mult))
                    dve.tensor_reduce(var[:, :], sq[:, :, :], X, ALU.add).then_inc(s_var, 1)
                    dve.wait_ge(s_sd, 1)
                    link(dve.reciprocal(mean[:, :], dev[:, :]))
                    link(dve.tensor_tensor(Hs[:, :, :], Hs[:, :, :], mean[:, :].unsqueeze(2).to_broadcast(wide3), ALU.mult))
                    dve.tensor_scalar(Hs[:, :, :], Hs[:, :, :], 0.0, None, ALU.max)

                @block.scalar
                def _(act):
                    act.wait_ge(s_var, 1)
                    act.activation(dev[:, :], var[:, :], ACT.Sqrt, bias=eps[:, 0:1], scale=1.0 / D).then_inc(s_sd, 1)

        def node_rows(table, row):
            return table.rearrange("(b p) w -> p b w", p=P)

        def store(pairs, c, name):
            s = sem(name, c)
            with nc.Block() as block:
                @block.sync
                def _(sp):
                    for to, of in pairs:
                        sp.dma_start(to.rearrange("(b p) w -> p b w", p=P), of).then_inc(s, 16)
                    sp.wait_ge(s, 16 * len(pairs))

        def diagonal(c, name, weights, R, width):
            rows = P // R
            t = sb(name, [P, R * width], F32, c)
            s0, s1 = sem(name + "_0", c), sem(name + "_1", c)
            with nc.Block() as block:
                @block.vector
                def _(dve):
                    dve.memset(t[:, :], 0.0).then_inc(s0, 1)

                @block.sync
                def _(sp):
                    sp.wait_ge(s0, 1)
                    for r in range(R):
                        for at, w in weights:
                            sp.dma_start(t[r * rows:(r + 1) * rows, r * width + at:r * width + at + w.shape[1]], w).then_inc(s1, 16)
                    sp.wait_ge(s1, R * len(weights) * 16)
            return t

        def bias_rows(c, name, items, width, R):
            t = sb(name, [1, R, width], F32, c)
            s1 = sem(name + "_1", c)
            with nc.Block() as block:
                @block.sync
                def _(sp):
                    for r in range(R):
                        for at, w in items:
                            sp.dma_start(t[0:1, r, at:at + w.shape[0]], w.unsqueeze(0)).then_inc(s1, 16)
                    sp.wait_ge(s1, R * len(items) * 16)
            return t[:, :, :].rearrange("a r w -> a (r w)")

        def node_matmul(name, c, steps, take, weights, bias, put, hidden=None):
            W = weights.shape[1]
            part = [sb(f"part{u}", [P, P], F32, c) for u in range(2)]
            turned = [sb(f"turned{u}", [P, P], F32, c) for u in range(2)]
            hid = [sb(f"hid{u}", [P, P], F32, c) for u in range(2)] if hidden else turned
            s_part, s_tr, s_in, s_h, s_hr, s_mm, s_out = (sem(name + n, c) for n in ("part", "tr", "in", "h", "hr", "mm", "out"))
            with nc.Block() as block:
                @block.vector
                def _(dve):
                    for step in group_steps(dve, steps, 2, 2):
                        at = step(0)
                        if at:
                            if not at.first:
                                dve.wait_ge(s_tr, at.g - 1)
                            take(dve, at.g, part[at.slot]).then_inc(s_part, 1)
                        at = step(2)
                        if at:
                            dve.wait_ge(s_mm, at.g + 1)
                            put(dve, at.g, psum[4 + at.slot][:, 0:W]).then_inc(s_out, 1)

                @block.scalar
                def _(act):
                    for step in group_steps(act, steps, 2, 1):
                        at = step(0)
                        if at:
                            if not at.first:
                                act.wait_ge(s_h if hidden else s_mm, at.g - 1)
                            act.wait_ge(s_tr, at.g + 1)
                            act.activation(turned[at.slot][:, :], psum[at.slot][:, 0:P], ACT.Copy).then_inc(s_in, 1)
                        at = step(1)
                        if at and hidden:
                            if not at.first:
                                act.wait_ge(s_mm, at.g - 1)
                            act.wait_ge(s_h, at.g + 1)
                            act.activation(hid[at.slot][:, :], psum[2 + at.slot][:, 0:P], ACT.Relu, bias=hidden[1][:, 0:1]).then_inc(s_hr, 1)

                @block.tensor
                def _(pe):
                    for step in group_steps(pe, steps, 2, 1):
                        at = step(0)
                        if at:
                            if not at.first:
                                pe.wait_ge(s_in, at.g - 1)
                            pe.wait_ge(s_part, at.g + 1)
                            pe.transpose(psum[at.slot][:, 0:P], part[at.slot][:, :], ident[:, :]).then_inc(s_tr, 1)
                        at = step(1)
                        if at:
                            if hidden:
                                pe.wait_ge(s_in, at.g + 1)
                                if not at.first:
                                    pe.wait_ge(s_hr, at.g - 1)
                                pe.matmul(psum[2 + at.slot][:, 0:P], hidden[0][:, :], turned[at.slot][:, :], start=True, stop=True)\
                                  .then_inc(s_h, 1)
                            pe.wait_ge(s_hr if hidden else s_in, at.g + 1)
                            if not at.first:
                                pe.wait_ge(s_out, at.g - 1)
                            if bias is not None:
                                pe.matmul(psum[4 + at.slot][:, 0:W], onesf[:, :], bias, start=True, stop=False)
                            pe.matmul(psum[4 + at.slot][:, 0:W], hid[at.slot][:, :], weights, start=bias is None, stop=True)\
                              .then_inc(s_mm, 1)

        def three_parts(dve, link, parts, whole, rest):
            link(dve.tensor_copy(parts[0], whole))
            link(dve.tensor_tensor(rest, whole, parts[0], ALU.subtract))
            link(dve.tensor_copy(parts[1], rest))
            link(dve.tensor_tensor(rest, rest, parts[1], ALU.subtract))
            link(dve.tensor_copy(parts[2], rest))

        class Pass:

            def __init__(self, name, c, k, depth, width, table, local=None):
                self.name, self.c, self.k, self.depth, self.width, self.table, self.local = name, c, k, depth, width, table, local
                self.sem = lambda n: sem(f"{name}_{n}", c)
                self.sb = lambda n, shape, dt: sb(f"{name}_{n}", shape, dt, c)
                self.ring = lambda n, shape, dt, depth=depth: [sb(f"{name}_{n}{u}", shape, dt, c) for u in range(depth)]
                self.list = self.ring("list", [P, T], I32)
                self.oe = self.ring("oe", [P, T, P], F32)
                self.listed = [self.sem(f"listed{u}") for u in range(depth)]
                self.base = list(pool_base)
                for u in range(depth):
                    pool_base[u] += NG // depth * T * 16
                self.loaded = [self.sem(f"loaded{u}") for u in range(depth)]
                self.hot, self.summed, self.done, self.go = (self.sem(n) for n in ("hot", "summed", "done", "go"))
                if local is not None:
                    self.row = self.ring("row", [P, GE], BF16)
                    self.ot = self.ring("ot", [P, GE], BF16)
                    self.loc = self.ring("loc", [P, local.shape[1]], BF16)

            def load(self, sp, at, feats=None):
                if not at.first:
                    sp.wait_ge(self.done, at.g - (self.depth - 1))
                u = at.slot
                sp.dma_start(self.list[u][:, :], idx[self.k][:, ds(at.g * T, T)]).then_inc(self.listed[u], 16)
                n = 0
                if self.local is not None:
                    sp.dma_start(self.row[u][:, :], rowT[self.k][ds(at.g * T, T), :].rearrange("t p -> (t p)").unsqueeze(0)
                                 .to_broadcast([P, GE])).then_inc(self.loaded[u], 16)
                    b = sp.value_load(blk[self.k][0:1, ds(at.g, 1)], min_val=0, max_val=NB - 1)
                    sp.dma_start(self.loc[u][:, :], self.local[ds(b * P, P), :]).then_inc(self.loaded[u], 16)
                    n = 2
                if feats is not None:
                    view = rec[self.k].bitcast(F32).rearrange("(g p j) w -> g p j w", p=P, j=T)
                    sp.dma_start(feats[u], view[ds(at.g, 1), :, :, 2:RW].rearrange("a p j w -> (a p) j w")).then_inc(self.loaded[u], 16)
                    n += 1
                self.loads = n

            def gather(self, pool, at, to):
                u = at.slot
                pool.wait_ge(self.listed[u], (at.turn + 1) * 16)
                if not at.first:
                    pool.wait_ge(self.done, at.g - (self.depth - 1))
                pool.sem_inc(self.go, 1)
                for j in range(T):
                    pool.indirect_dma_start(to[u][:, j, 0:self.width], None, self.table,
                                            bass.IndirectOffsetOnAxis(ap=self.list[u][:, j:j + 1], axis=0)).then_inc(pool_dma[u], 16)

            def rows_here(self, at):
                return (at.turn + 1) * (16 * T) + self.base[at.slot]

            def edges_hot(self, dve, at):
                u = at.slot
                if self.local is not None:
                    dve.wait_ge(self.loaded[u], (at.turn + 1) * 16 * self.loads)
                    dve.tensor_scalar(self.ot[u][:, :], self.row[u][:, :], iop[:, 0:1], None, ALU.is_equal)
                dve.tensor_tensor(self.oe[u][:, :, :], iof[:, :].unsqueeze(1).to_broadcast([P, T, P]),
                                  near[self.k][:, ds(at.g * T, T)].unsqueeze(2).to_broadcast([P, T, P]), ALU.is_equal).then_inc(self.hot, 1)

            def segment_sum(self, pe, at, values, width):
                if not (isinstance(at.g, int) and at.g < 2):
                    pe.wait_ge(self.done, at.g - 1)
                bank = psum[6 + at.slot % 2][:, 0:width]
                for j in range(T):
                    ins = pe.matmul(bank, self.oe[at.slot][:, j, :], values(j), start=j == 0, stop=j == T - 1)
                ins.then_inc(self.summed, 1)

            def block_of(self, eng, at):
                return eng.value_load(blk[self.k][0:1, ds(at.g, 1)], min_val=0, max_val=NB - 1)

            def add(self, dve, at, acc, width):
                dve.wait_ge(self.summed, at.g + 1)
                if not (isinstance(at.g, int) and at.g == 0):
                    dve.wait_ge(self.done, at.g)
                b = self.block_of(dve, at)
                mine = acc[:, ds(b, 1), :].rearrange("p a w -> p (a w)")
                dve.tensor_tensor(mine, mine, psum[6 + at.slot % 2][:, 0:width], ALU.add).then_inc(self.done, 1)

        def update(dve, i, R, value):
            mine = Xs[:, ds(i * R, R), :].rearrange("p r f -> p (r f)")
            return mine

        with Scope() as c:
            normalise(c)
            acc = sb("acc0", [P, NBP, D + 1], F32, c)
            store([(gath[0], Hs[:, :, :])], c, "st0")
            ps = Pass("l0", c, 0, U, D, gath[0])
            feat = ps.ring("feat", [P, T, D + 1], F32)
            s_one, s_acc0 = sem("s_one", c), sem("s_acc0", c)
            with nc.Block() as block:
                @block.sync
                def _(sp):
                    for step in group_steps(sp, NG, ps.depth, 0):
                        ps.load(sp, step(0))

                @block.gpsimd
                def _(pool):
                    for step in group_steps(pool, NG, ps.depth, 0):
                        ps.gather(pool, step(0), feat)

                @block.tensor
                def _(pe):
                    pe.wait_ge(s_one, 1)
                    for step in group_steps(pe, NG, ps.depth, 0):
                        at = step(0)
                        pe.wait_ge(ps.hot, at.g + 1)
                        pe.wait_ge(pool_dma[at.slot], ps.rows_here(at))
                        ps.segment_sum(pe, at, lambda j: feat[at.slot][:, j, :], D + 1)

                @block.vector
                def _(dve):
                    for u in range(ps.depth):
                        dve.memset(feat[u][:, :, D:D + 1], 1.0)
                    dve.memset(acc[:, :, :], 0.0).then_inc(s_one, 1)
                    dve.wait_ge(s_one, 1)
                    for step in group_steps(dve, NG, ps.depth, 1):
                        if at := step(0):
                            ps.edges_hot(dve, at)
                        if at := step(1):
                            ps.add(dve, at, acc, D + 1)

            both = sb("both0", [P, NBP, 2 * D], F32, c)
            count = sb("count", [P, NBP], F32, c)
            with nc.Block() as block:
                @block.vector
                def _(dve):
                    link = chained(dve, "chain_0", c)
                    link(dve.tensor_scalar(count[:, :], acc[:, :, D], 1.0, None, ALU.max))
                    link(dve.reciprocal(count[:, :], count[:, :]))
                    dve.tensor_copy(both[:, :, 0:D], Hs[:, :, :])
                    dve.tensor_tensor(both[:, :, D:2 * D], acc[:, :, 0:D], count[:, :].unsqueeze(2).to_broadcast([P, NBP, D]), ALU.mult)
            w = diagonal(c, "w0", [(0, W0)], 2, D)
            bias = bias_rows(c, "bias0", [(0, b0)], D, 2)

            def put0(dve, i, value):
                mine = Xs[:, ds(i * 2, 2), :].rearrange("p r f -> p (r f)")
                return dve.scalar_tensor_tensor(mine, value, 0.0, mine, ALU.max, ALU.add)
            node_matmul("n0", c, NBP // 2, lambda dve, i, to: dve.tensor_copy(to[:, :].rearrange("p (r f) -> p r f", r=2), both[:, ds(i * 2, 2), :]),
                        w[:, :], bias, put0)

        def softmax_pass(name, c, k, width, table, local, heads_w, acc, best, scores_in, score, spread):
            ps = Pass(name, c, k, 8, width, table, local)
            W = HEADS * heads_w
            far = ps.ring("far", [P, T, width], F32)
            sc = ps.ring("sc", [P, T, HEADS], F32)
            turned = ps.ring("turned", [HEADS, GE], BF16, 2)
            top = ps.sb("top", [P, HEADS], F32)
            new = ps.ring("new", [P, HEADS], BF16)
            fall = ps.ring("fall", [P, HEADS], F32)
            keep = ps.ring("keep", [P, HEADS], F32)
            under = ps.ring("under", [P, T, HEADS], F32)
            val = ps.ring("val", [P, T, HEADS, heads_w], F32)
            (s_near, s_tmp, s_sc, s_turn, s_turned, s_cast, s_top, s_new, s_fall, s_best, s_keep, s_atedge, s_under, s_weight,
             s_val, s_kept, s_init) = (ps.sem(n) for n in (
                 "near", "tmp", "sc", "turn", "turned", "cast", "top", "new", "fall", "best", "keep", "atedge", "under", "weight",
                 "val", "kept", "init"))

            def at_edge(at):
                return psum[6 + at.slot % 2][:, 384:384 + T * HEADS]

            with nc.Block() as block:
                @block.sync
                def _(sp):
                    for step in group_steps(sp, NG, ps.depth, 0):
                        ps.load(sp, step(0))

                @block.gpsimd
                def _(pool):
                    for step in group_steps(pool, NG, ps.depth, 0):
                        ps.gather(pool, step(0), far)

                @block.vector
                def _(dve):
                    dve.memset(best[:, :, :], NONE).then_inc(s_init, 1)
                    dve.memset(acc[:, :, :], 0.0).then_inc(s_init, 1)
                    dve.wait_ge(s_init, 2)
                    for step in group_steps(dve, NG, ps.depth, 3):
                        if at := step(2):
                            dve.wait_ge(s_cast, at.g + 1)
                            dve.tensor_reduce(top[:, :], wide[:, :, :], X, ALU.max).then_inc(s_top, 1)
                            b = ps.block_of(dve, at)
                            mine = best[:, ds(b, 1), :].rearrange("p a h -> p (a h)")
                            dve.wait_ge(s_top, at.g + 1)
                            if not (isinstance(at.g, int) and at.g == 0):
                                dve.wait_ge(s_best, at.g)
                            dve.scalar_tensor_tensor(new[at.slot][:, :], top[:, :], BIG, mine, ALU.subtract, ALU.max).then_inc(s_new, 1)
                            dve.wait_ge(s_new, at.g + 1)
                            dve.tensor_tensor(fall[at.slot][:, :], mine, new[at.slot][:, :], ALU.subtract).then_inc(s_fall, 1)
                            dve.wait_ge(s_fall, at.g + 1)
                            dve.tensor_scalar(mine, new[at.slot][:, :], NONE, None, ALU.max).then_inc(s_best, 1)
                        if at := step(1):
                            dve.wait_ge(s_near, at.g + 1)
                            dve.wait_ge(pool_dma[at.slot], ps.rows_here(at))
                            score(dve, at, far, sc[at.slot], s_tmp, s_sc)
                        if at := step(2):
                            dve.wait_ge(s_atedge, at.g + 1)
                            dve.tensor_tensor(under[at.slot][:, :, :], sc[at.slot][:, :, :],
                                              at_edge(at).rearrange("p (j h) -> p j h", h=HEADS), ALU.subtract).then_inc(s_under, 1)
                        if at := step(0):
                            ps.edges_hot(dve, at)
                        if at := step(2):
                            dve.wait_ge(s_weight, at.g + 1)
                            spread(dve, far[at.slot], val[at.slot]).then_inc(s_val, 1)
                        if at := step(3):
                            b = ps.block_of(dve, at)
                            mine = acc[:, ds(b, 1), :].rearrange("p a w -> p (a w)")
                            heads = mine.rearrange("p (h w) -> p h w", h=HEADS)
                            dve.wait_ge(s_keep, at.g + 1)
                            if not (isinstance(at.g, int) and at.g == 0):
                                dve.wait_ge(ps.done, at.g)
                            dve.tensor_tensor(heads, heads, keep[at.slot][:, :].unsqueeze(2).to_broadcast([P, HEADS, heads_w]),
                                              ALU.mult).then_inc(s_kept, 1)
                            dve.wait_ge(ps.summed, at.g + 1)
                            dve.wait_ge(s_kept, at.g + 1)
                            dve.tensor_tensor(mine, mine, psum[6 + at.slot % 2][:, 0:W], ALU.add).then_inc(ps.done, 1)

                @block.scalar
                def _(act):
                    for step in group_steps(act, NG, ps.depth, 2):
                        if at := step(2):
                            act.wait_ge(s_fall, at.g + 1)
                            act.activation(keep[at.slot][:, :], fall[at.slot][:, :], ACT.Exp).then_inc(s_keep, 1)
                        if at := step(1):
                            if not (isinstance(at.g, int) and at.g < 2):
                                act.wait_ge(s_cast, at.g - 1)
                            act.wait_ge(s_turn, at.g + 1)
                            act.activation(turned[at.slot % 2][:, :], psum[1][0:HEADS, :], ACT.Copy).then_inc(s_turned, 1)
                        if at := step(2):
                            act.wait_ge(s_under, at.g + 1)
                            act.activation(val[at.slot][:, :, :, heads_w - 1], under[at.slot][:, :, :], ACT.Exp).then_inc(s_weight, 1)

                @block.tensor
                def _(pe):
                    for step in group_steps(pe, NG, ps.depth, 2):
                        if at := step(2):
                            pe.wait_ge(s_new, at.g + 1)
                            for j in range(T):
                                ins = pe.matmul(at_edge(at)[:, j * HEADS:(j + 1) * HEADS], ps.ot[at.slot][:, j * P:(j + 1) * P],
                                                new[at.slot][:, :], start=True, stop=True)
                            ins.then_inc(s_atedge, 1)
                        if at := step(1):
                            pe.wait_ge(s_sc, at.g + 1)
                            if not (isinstance(at.g, int) and at.g == 0):
                                pe.wait_ge(s_turned, at.g)
                            for j in range(T):
                                ins = pe.transpose(psum[1][0:HEADS, j * P:(j + 1) * P], sc[at.slot][:, j, :], ident[:, :])
                            ins.then_inc(s_turn, 1)
                        if at := step(0):
                            pe.wait_ge(ps.hot, at.g + 1)
                            scores_in(pe, at, ps).then_inc(s_near, 1)
                        if at := step(1):
                            pe.wait_ge(s_turned, at.g + 1)
                            if not (isinstance(at.g, int) and at.g == 0):
                                pe.wait_ge(s_top, at.g)
                            for h in range(HEADS):
                                pe.matmul(wide[:, h, :], bigI[:, :], ps.ot[at.slot][:, :], start=True, stop=False)
                                ins = pe.matmul(wide[:, h, :], sel[:, h, :], turned[at.slot % 2][:, :], start=False, stop=True)
                            ins.then_inc(s_cast, 1)
                        if at := step(2):
                            pe.wait_ge(s_val, at.g + 1)
                            ps.segment_sum(pe, at, lambda j: val[at.slot][:, j, :, :].rearrange("p h w -> p (h w)"), W)

        def near_part(width):
            def run(pe, at, ps):
                for j in range(T):
                    for i in range(3):
                        ins = pe.matmul(psum[0][:, j * width:(j + 1) * width], ps.ot[at.slot][:, j * P:(j + 1) * P],
                                        ps.loc[at.slot][:, i * width:(i + 1) * width], start=i == 0, stop=i == 2)
                return ins
            return run

        with Scope() as c:
            normalise(c)
            tab = sb("tab1", [P, NBP, 3 * D], F32, c)
            w = diagonal(c, "w1", [(0, Wq), (D, Wk), (2 * D, Wv)], 4, 3 * D)
            node_matmul("n1", c, NBP // 4, lambda dve, i, to: dve.tensor_copy(to[:, :].rearrange("p (r f) -> p r f", r=4), Hs[:, ds(i * 4, 4), :]),
                        w[:, :], None, lambda dve, i, value: dve.tensor_copy(tab[:, ds(i * 4, 4), :].rearrange("p r w -> p (r w)"), value))
            with Scope() as c2:
                qs = sb("qs", [P, NBP, 3, D], BF16, c2)
                rest = sb("rest", [P, NBP, D], F32, c2)
                with nc.Block() as block:
                    @block.vector
                    def _(dve):
                        link = chained(dve, "chain_1", c2)
                        q = tab[:, :, 0:D]
                        link(dve.tensor_scalar(q, q, DH ** -0.5, None, ALU.mult))
                        three_parts(dve, link, [qs[:, :, i, :] for i in range(3)], q, rest[:, :, :])
                store([(locl[1], qs[:, :, :, :].rearrange("p b i w -> p b (i w)")), (gath[1], tab[:, :, D:3 * D])], c2, "st1")

        with Scope() as c:
            acc = sb("acc1", [P, NBP, D + HEADS], F32, c)
            best = sb("best1", [P, NBP, HEADS], F32, c)
            with Scope() as c2:
                prod = [sb(f"prod{u}", [P, T, D], F32, c2) for u in range(2)]

                def score1(dve, at, far, sc, s_tmp, s_sc):
                    dve.tensor_tensor(prod[at.slot % 2][:, :, :], psum[0][:, 0:T * D].rearrange("p (j w) -> p j w", j=T), far[at.slot][:, :, 0:D],
                                      ALU.mult).then_inc(s_tmp, 1)
                    dve.wait_ge(s_tmp, at.g + 1)
                    dve.tensor_reduce(sc[:, :, :], prod[at.slot % 2][:, :, :].rearrange("p j (h d) -> p j h d", d=DH), X, ALU.add).then_inc(s_sc, 1)

                def spread1(dve, far, val):
                    return dve.tensor_tensor(val[:, :, :, 0:DH], far[:, :, D:2 * D].rearrange("p j (h d) -> p j h d", d=DH),
                                             val[:, :, :, DH:DH + 1].to_broadcast([P, T, HEADS, DH]), ALU.mult)
                softmax_pass("l1", c2, 0, 2 * D, gath[1], locl[1], DH + 1, acc, best, near_part(D), score1, spread1)
            att = sb("att1", [P, NBP, D], F32, c)
            den = sb("den1", [P, NBP, HEADS], F32, c)
            with nc.Block() as block:
                @block.vector
                def _(dve):
                    link = chained(dve, "chain_1b", c)
                    a4 = acc[:, :, :].rearrange("p b (h w) -> p b h w", h=HEADS)
                    link(dve.tensor_scalar(den[:, :, :], a4[:, :, :, DH], 1e-16, None, ALU.max))
                    link(dve.reciprocal(den[:, :, :], den[:, :, :]))
                    dve.tensor_tensor(att[:, :, :].rearrange("p b (h d) -> p b h d", h=HEADS), a4[:, :, :, 0:DH],
                                      den[:, :, :].unsqueeze(3).to_broadcast([P, NBP, HEADS, DH]), ALU.mult)
                    dve.tensor_tensor(Xs[:, :, :], Xs[:, :, :], Hs[:, :, :], ALU.add)
            w = diagonal(c, "wo", [(0, Wo)], 4, D)

            def add_rows(R):
                def put(dve, i, value):
                    mine = Xs[:, ds(i * R, R), :].rearrange("p r f -> p (r f)")
                    return dve.tensor_tensor(mine, mine, value, ALU.add)
                return put
            node_matmul("n1b", c, NBP // 4, lambda dve, i, to: dve.tensor_copy(to[:, :].rearrange("p (r f) -> p r f", r=4), att[:, ds(i * 4, 4), :]),
                        w[:, :], None, add_rows(4))

        with Scope() as c:
            normalise(c)
            tab = sb("tab2", [P, NBP, 2 * H2], F32, c)
            w = diagonal(c, "w2", [(0, W1f[0:D, :]), (H2, W1b[0:D, :])], 4, 2 * H2)
            bias = bias_rows(c, "bias2", [(0, b1f), (H2, b1b)], 2 * H2, 4)
            node_matmul("n2", c, NBP // 4, lambda dve, i, to: dve.tensor_copy(to[:, :].rearrange("p (r f) -> p r f", r=4), Hs[:, ds(i * 4, 4), :]),
                        w[:, :], bias, lambda dve, i, value: dve.tensor_copy(tab[:, ds(i * 4, 4), :].rearrange("p r w -> p (r w)"), value))
            store([(gath[2], Hs[:, :, :])], c, "st2")
            us = sb("us", [P, NBP, 3, H2], BF16, c)
            rest = sb("rest2", [P, NBP, H2], F32, c)
            for way, to in ((0, locl[2]), (1, locl[4])):
                with nc.Block() as block:
                    @block.vector
                    def _(dve):
                        link = chained(dve, f"chain_2{way}", c)
                        three_parts(dve, link, [us[:, :, i, :] for i in range(3)], tab[:, :, way * H2:(way + 1) * H2], rest[:, :, :])
                store([(to, us[:, :, :, :].rearrange("p b i w -> p b (i w)"))], c, f"st2{way}")

        def flow_pass(name, c, k, local, W1, W2, b2, acc, first):
            FW = D + DE
            ps = Pass(name, c, k, U, D, gath[2], local)
            feat = ps.ring("feat", [P, T, FW], F32)
            featT = ps.ring("featT", [FW, GE], F32, 2)
            hid = ps.ring("hid", [H2, GE], F32, 2)
            msg = ps.ring("msg", [P, T * D], F32, 2)
            w1 = ps.sb("w1", [FW, H2], F32)
            w2 = ps.sb("w2", [H2, D], F32)
            b2r = bias_rows(c, name + "b2r", [(0, b2)], D, 1)
            s_w, s_zero, s_turn, s_turned, s_hid, s_rect, s_out, s_msg, s_carry = (ps.sem(n) for n in ("w", "zero", "turn", "turned", "hid", "rect", "out", "msg", "carry"))
            with nc.Block() as block:
                @block.sync
                def _(sp):
                    sp.dma_start(w1[:, :], W1[D:2 * D + DE, :]).then_inc(s_w, 16)
                    sp.dma_start(w2[:, :], W2).then_inc(s_w, 16)
                    for step in group_steps(sp, NG, ps.depth, 0):
                        ps.load(sp, step(0), [f[:, :, D:FW] for f in feat])

                @block.gpsimd
                def _(pool):
                    for step in group_steps(pool, NG, ps.depth, 0):
                        ps.gather(pool, step(0), feat)

                @block.vector
                def _(dve):
                    if first:
                        dve.memset(acc[:, :, :], 0.0).then_inc(s_zero, 1)
                        dve.wait_ge(s_zero, 1)
                    for step in group_steps(dve, NG, ps.depth, 1):
                        if at := step(0):
                            ps.edges_hot(dve, at)
                        if at := step(1):
                            ps.add(dve, at, acc[:, :, k * D:(k + 1) * D], D)

                @block.scalar
                def _(act):
                    for step in group_steps(act, NG, ps.depth, 1):
                        if at := step(0):
                            if not (isinstance(at.g, int) and at.g < 2):
                                act.wait_ge(s_hid, at.g - 1)
                            act.wait_ge(s_turn, at.g + 1)
                            act.activation(featT[at.slot % 2][:, :], psum[0][0:FW, :], ACT.Copy).then_inc(s_turned, 1)
                        if at := step(1):
                            if not (isinstance(at.g, int) and at.g < 2):
                                act.wait_ge(ps.summed, at.g - 1)
                            act.wait_ge(s_out, at.g + 1)
                            act.activation(msg[at.slot % 2][:, :], psum[3][:, 0:T * D], ACT.Relu).then_inc(s_msg, 1)
                        if at := step(0):
                            if not (isinstance(at.g, int) and at.g < 2):
                                act.wait_ge(s_out, at.g - 1)
                            act.wait_ge(s_hid, at.g + 1)
                            act.activation(hid[at.slot % 2][:, :], psum[2][0:H2, :], ACT.Relu).then_inc(s_rect, 1)

                @block.tensor
                def _(pe):
                    pe.wait_ge(s_w, 32)
                    for step in group_steps(pe, NG, ps.depth, 1):
                        if at := step(0):
                            pe.wait_ge(ps.loaded[at.slot], (at.turn + 1) * 16 * ps.loads)
                            pe.wait_ge(pool_dma[at.slot], ps.rows_here(at))
                            if not (isinstance(at.g, int) and at.g == 0):
                                pe.wait_ge(s_turned, at.g)
                            pe.sem_inc(s_carry, 1)
                            for j in range(T):
                                ins = pe.transpose(psum[0][0:FW, j * P:(j + 1) * P], feat[at.slot][:, j, :], ident[:, :])
                            ins.then_inc(s_turn, 1)
                        if at := step(1):
                            pe.wait_ge(s_rect, at.g + 1)
                            if not (isinstance(at.g, int) and at.g == 0):
                                pe.wait_ge(s_msg, at.g)
                            for j in range(T):
                                pe.matmul(psum[3][:, j * D:(j + 1) * D], onesf[:, :], b2r, start=True, stop=False)
                                ins = pe.matmul(psum[3][:, j * D:(j + 1) * D], hid[at.slot % 2][:, j * P:(j + 1) * P], w2[:, :],
                                                start=False, stop=True)
                            ins.then_inc(s_out, 1)
                        if at := step(0):
                            pe.wait_ge(ps.hot, at.g + 1)
                            if not (isinstance(at.g, int) and at.g == 0):
                                pe.wait_ge(s_rect, at.g)
                            for i in range(3):
                                pe.matmul(psum[2][0:H2, :], ps.loc[at.slot][:, i * H2:(i + 1) * H2], ps.ot[at.slot][:, :],
                                          start=i == 0, stop=False)
                            pe.wait_ge(s_turned, at.g + 1)
                            pe.sem_inc(s_carry, 1)
                            pe.matmul(psum[2][0:H2, :], w1[:, :], featT[at.slot % 2][:, :], start=False, stop=True).then_inc(s_hid, 1)
                        if at := step(1):
                            pe.wait_ge(s_msg, at.g + 1)
                            ps.segment_sum(pe, at, lambda j: msg[at.slot % 2][:, j * D:(j + 1) * D], D)

        with Scope() as c:
            flows = sb("flows", [P, NBP, 2 * D], F32, c)
            with Scope() as c2:
                flow_pass("l2f", c2, 0, locl[2], W1f, W2f, b2f, flows, True)
            with Scope() as c2:
                flow_pass("l2b", c2, 1, locl[4], W1b, W2b, b2b, flows, False)
            w1n = diagonal(c, "w1n", [(0, W1n)], 2, H2)
            w2n = diagonal(c, "w2n", [(0, W2n)], 2, D)
            b1c = sb("b1c", [P, 1], F32, c)
            s_b1 = sem("s_b1", c)
            with nc.Block() as block:
                @block.sync
                def _(sp):
                    for r in range(2):
                        sp.dma_start(b1c[r * H2:(r + 1) * H2, :], b1n.unsqueeze(1)).then_inc(s_b1, 16)
                    sp.wait_ge(s_b1, 32)
            bias = bias_rows(c, "bias2n", [(0, b2n)], D, 2)
            node_matmul("n2n", c, NBP // 2, lambda dve, i, to: dve.tensor_copy(to[:, :].rearrange("p (r f) -> p r f", r=2), flows[:, ds(i * 2, 2), :]),
                        w2n[:, :], bias, put0, hidden=(w1n, b1c))

        with Scope() as c:
            normalise(c)
            tab = sb("tab3", [P, NBP, 2 * HEADS], F32, c)
            w = sb("w3a", [P, 4, 4 * HEADS * 2 // 4], F32, c)
            w3r = sb("w3r", [P, HEADS, D], F32, c)
            fcr = sb("fcr", [P, 2, D], F32, c)
            prod3 = sb("prod3", [P, HEADS, D], F32, c)
            col = sb("col3", [P, 2, HEADS], F32, c)
            bias = sb("bias3a", [1, 4, 2, HEADS], F32, c)
            fcb = sb("fcb", [1, 1], F32, c)
            s_w3 = sem("s_w3", c)
            with nc.Block() as block:
                @block.sync
                def _(sp):
                    for r in range(4):
                        sp.dma_start(w3r[r * D:(r + 1) * D, :, :], w3.rearrange("h f o -> f h o")).then_inc(s_w3, 16)
                    sp.dma_start(fcr[:, :, :].rearrange("p a o -> p (a o)"), fc_w[0:1, :].to_broadcast([P, 2 * D])).then_inc(s_w3, 16)
                    sp.dma_start(fcb[:, :], fc_b.unsqueeze(0)).then_inc(s_w3, 16)

                @block.vector
                def _(dve):
                    link = chained(dve, "chain_3", c)
                    link(dve.memset(w[:, :, :], 0.0))
                    link(dve.memset(bias[:, :, :, :], 0.0))
                    dve.wait_ge(s_w3, 96)
                    for a in range(2):
                        link(dve.tensor_tensor(prod3[:, :, :], w3r[:, :, :], fcr[:, a:a + 1, :].to_broadcast([P, HEADS, D]), ALU.mult))
                        link(dve.tensor_reduce(col[:, a, :], prod3[:, :, :], X, ALU.add))
                    for r in range(4):
                        link(dve.tensor_copy(w[r * D:(r + 1) * D, r, :], col[r * D:(r + 1) * D, :, :].rearrange("p a h -> p (a h)")))
                    link(dve.tensor_scalar(bias[:, :, 0, :], bias[:, :, 0, :], fcb[0:1, 0:1], None, ALU.add))
            node_matmul("n3", c, NBP // 4, lambda dve, i, to: dve.tensor_copy(to[:, :].rearrange("p (r f) -> p r f", r=4), Hs[:, ds(i * 4, 4), :]),
                        w[:, :, :].rearrange("p r w -> p (r w)"), bias[:, :, :, :].rearrange("a r k h -> a (r k h)"),
                        lambda dve, i, value: dve.tensor_copy(tab[:, ds(i * 4, 4), :].rearrange("p r w -> p (r w)"), value))
            near3 = sb("near3", [P, NBP, 3, HEADS], BF16, c)
            rest = sb("rest3", [P, NBP, HEADS], F32, c)
            far3 = sb("far3", [P, NBP, D + HEADS], F32, c)
            with nc.Block() as block:
                @block.vector
                def _(dve):
                    link = chained(dve, "chain_3b", c)
                    three_parts(dve, link, [near3[:, :, i, :] for i in range(3)], tab[:, :, 0:HEADS], rest[:, :, :])
                    dve.tensor_copy(far3[:, :, 0:D], Hs[:, :, :])
                    dve.tensor_copy(far3[:, :, D:D + HEADS], tab[:, :, HEADS:2 * HEADS])
            store([(locl[3], near3[:, :, :, :].rearrange("p b i w -> p b (i w)")), (gath[3], far3[:, :, :])], c, "st3")

        with Scope() as c:
            HW = D + 1
            acc = sb("acc3", [P, NBP, HEADS * HW], F32, c)
            best = sb("best3", [P, NBP, HEADS], F32, c)
            with Scope() as c2:
                raw = [sb(f"raw{u}", [P, T, HEADS], F32, c2) for u in range(2)]

                def score3(dve, at, far, sc, s_tmp, s_sc):
                    r = raw[at.slot % 2]
                    dve.tensor_tensor(r[:, :, :], psum[0][:, 0:T * HEADS].rearrange("p (j h) -> p j h", j=T), far[at.slot][:, :, D:D + HEADS],
                                      ALU.add).then_inc(s_tmp, 1)
                    dve.wait_ge(s_tmp, at.g + 1)
                    dve.scalar_tensor_tensor(sc[:, :, :], r[:, :, :], 0.2, r[:, :, :], ALU.mult, ALU.max).then_inc(s_sc, 1)

                def spread3(dve, far, val):
                    return dve.tensor_tensor(val[:, :, :, 0:D], far[:, :, 0:D].unsqueeze(2).to_broadcast([P, T, HEADS, D]),
                                             val[:, :, :, D:D + 1].to_broadcast([P, T, HEADS, D]), ALU.mult)
                softmax_pass("l3", c2, 1, D + HEADS, gath[3], locl[3], HW, acc, best, near_part(HEADS), score3, spread3)
            den = sb("den3", [P, NBP, HEADS], F32, c)
            w = sb("w3b", [P, D], F32, c)
            s_w3b = sem("s_w3b", c)
            with nc.Block() as block:
                @block.sync
                def _(sp):
                    sp.dma_start(w[:, :], w3.rearrange("h f o -> (h f) o")).then_inc(s_w3b, 16)

                @block.vector
                def _(dve):
                    link = chained(dve, "chain_3c", c)
                    a4 = acc[:, :, :].rearrange("p b (h w) -> p b h w", h=HEADS)
                    link(dve.tensor_scalar(den[:, :, :], a4[:, :, :, D], 1e-30, None, ALU.max))
                    link(dve.reciprocal(den[:, :, :], den[:, :, :]))
                    dve.tensor_tensor(a4[:, :, :, 0:D], a4[:, :, :, 0:D], den[:, :, :].unsqueeze(3).to_broadcast([P, NBP, HEADS, D]), ALU.mult)
                    dve.wait_ge(s_w3b, 16)
                    dve.tensor_scalar(w[:, :], w[:, :], 1.0 / HEADS, None, ALU.mult)
            bias = bias_rows(c, "bias3", [(0, bias3)], D, 1)
            node_matmul("n3b", c, NBP,
                        lambda dve, i, to: dve.tensor_copy(to[:, :].rearrange("p (h f) -> p h f", h=HEADS),
                                                           acc[:, ds(i, 1), :].rearrange("p a (h w) -> p (a h) w", h=HEADS)[:, :, 0:D]),
                        w[:, :], bias, add_rows(1))
            s_res = sem("s_res", c)
            with nc.Block() as block:
                @block.sync
                def _(sp):
                    sp.dma_start(out[0:FULL * P, :].rearrange("(b p) f -> p b f", p=P), Xs[:, 0:FULL, :]).then_inc(s_res, 16)
                    sp.dma_start(out[FULL * P:N, :], Xs[0:N - FULL * P, FULL, :]).then_inc(s_res, 16)
                    sp.wait_ge(s_res, 32)


_INS = ['x', 'src', 'dst', 'edge_attr_16', 'L0_gnn_W', 'L0_gnn_b', 'L1_gnn_Wq', 'L1_gnn_Wk', 'L1_gnn_Wv', 'L1_gnn_Wo',
        'L2_gnn_W1f', 'L2_gnn_b1f', 'L2_gnn_W2f', 'L2_gnn_b2f', 'L2_gnn_W1b', 'L2_gnn_b1b', 'L2_gnn_W2b', 'L2_gnn_b2b',
        'L2_gnn_W1n', 'L2_gnn_b1n', 'L2_gnn_W2n', 'L2_gnn_b2n', 'L3_gnn_w', 'L3_gnn_fc_w', 'L3_gnn_fc_b', 'L3_gnn_bias']


def kernel(**inputs):
    import numpy as _np
    import concourse.bacc as _bacc
    from concourse import mybir as _mybir
    from concourse.bass_utils import run_bass_kernel_spmd as _run

    nc = _bacc.Bacc("TRN2", target_bir_lowering=False, num_devices=1)
    arrays, args = {}, []
    for name in _INS:
        a = _np.ascontiguousarray(inputs[name])
        arrays[f"in_{name}_dram"] = a
        args.append(nc.dram_tensor(f"in_{name}_dram", a.shape, _mybir.dt.from_np(a.dtype), kind="ExternalInput").ap())
    args.append(nc.dram_tensor("out_dram", (N, D), _mybir.dt.float32, kind="ExternalOutput").ap())
    gnn_kernel(nc, *args)
    r = _run(nc, [arrays], core_ids=[0])
    return r.results[0]["out_dram"]
```

```python
import concourse.bass as bass
from concourse import mybir
from contextlib import ExitStack

F32 = mybir.dt.float32
BF16 = mybir.dt.bfloat16
I16 = mybir.dt.int16
I32 = mybir.dt.int32
ALU = mybir.AluOpType
ACT = mybir.ActivationFunctionType
X = mybir.AxisListType.X
ds = bass.ds

N, E, D, DE = 12500, 200000, 32, 16
P = 128
NB = (N + P - 1) // P
FULL = N // P
NBP = (NB + 7) // 8 * 8
NP = NBP * P
HEADS, DH, H2 = 4, 8, 64
EP = 125
EC = E // EP
CB = 5
T = 4
GE = T * P
U = 8
CH = -(-E // (GE * U)) * U
ER = CH * GE
NG = ((E - NB) // GE + NB + U - 1) // U * U
GP = max(d for d in range(1, P + 1) if NG % d == 0)
GQ = NG // GP
RW = 2 + DE
TR = max(d for d in range(1, P + 1) if CH % d == 0)
CG = max(d for d in range(1, 65) if CH % d == 0)
BIG = float(2 ** 20)
CS, CR, RR = EC // NG, 8, 4
RS = (EC - CH * CS) // CR
RF = RS - (NG - CH) // U * RR
assert CH * CS + RS * CR == EC and RF >= 0
NONE = -2.0 * BIG


class At:

    def __init__(self, g, slot, turn):
        self.g, self.slot, self.turn = g, slot, turn
        self.first = isinstance(turn, int) and turn == 0


def group_steps(eng, groups, depth, lag, peel=1):
    for t in range(peel * depth):
        yield lambda k, t=t: At(t - k, (t - k) % depth, (t - k) // depth) if t >= k else None
    with eng.Fori(peel, groups // depth) as i:
        for u in range(depth):
            yield lambda k, u=u: At(i * depth + (u - k), (u - k) % depth, i + (u - k) // depth)
    for t in range(groups, groups + lag):
        yield lambda k, t=t: At(t - k, (t - k) % depth, (t - k) // depth) if t - k < groups else None


def gnn_kernel(nc, x, src, dst, edge_attr, W0, b0, Wq, Wk, Wv, Wo, W1f, b1f, W2f, b2f, W1b, b1b, W2b, b2b,
               W1n, b1n, W2n, b2n, w3, fc_w, fc_b, bias3, out):
    ctx = ExitStack()
    with ctx:
        used = {}

        def unique(name):
            used[name] = used.get(name, 0) + 1
            return name if used[name] == 1 else f"{name}_{used[name]}"

        class Scope(ExitStack):
            sems = None

            def __exit__(self, *error):
                if self.sems and error[0] is None:
                    with nc.Block() as block:
                        @block.gpsimd
                        def _(pool):
                            for s in self.sems:
                                pool.sem_clear(s)
                return super().__exit__(*error)

        def sb(name, shape, dt, c=ctx):
            return c.enter_context(nc.sbuf_tensor(unique(name), shape, dt))

        def sem(name, c=ctx):
            s = c.enter_context(nc.semaphore(unique(name)))
            c.sems = (c.sems or []) + [s]
            return s

        def dram(name, shape, dt):
            return nc.dram_tensor(name, shape, dt).ap()

        low = ctx.enter_context(nc.psum_tensor("low", [P, 2, 512], F32))
        wide = ctx.enter_context(nc.psum_tensor("wide", [P, 4, 512], F32))
        high = ctx.enter_context(nc.psum_tensor("high", [P, 2, 512], F32))
        psum = [t[:, i, :] for t, n in ((low, 2), (wide, 4), (high, 2)) for i in range(n)]

        pool_dma = [ctx.enter_context(nc.semaphore(f"pool_dma{u}")) for u in range(8)]
        pool_base = [0] * 8
        pool_put = [ctx.enter_context(nc.semaphore(f"pool_put{u}")) for u in range(U)]

        rec = [dram(f"rec{k}", [ER, RW], I32) for k in range(2)]
        plain = dram("plain", [E, RW + 1], I32)
        keys = [dram(f"keys{k}", [ER], I16) for k in range(2)]
        plan_d = [dram(f"plan{k}", [3, NG], I32) for k in range(2)]
        rows = [dram(f"rows{i}", [ER, w], t) for i, (w, t) in enumerate(
            ((3 * D, BF16), (2 * D, F32), (D, F32), (D + HEADS, F32), (D, F32)))]
        gath = [dram(f"gath{i}", [NP, w], t) for i, (w, t) in enumerate(((3 * D, BF16), (2 * D, F32), (D, F32), (D + HEADS, F32)))]
        locl = [None, dram("locl1", [NP, 3 * D], BF16), dram("locl2f", [NP, 3 * H2], BF16),
                dram("locl3", [NP, 3 * HEADS], BF16), dram("locl2b", [NP, 3 * H2], BF16)]

        Xs = sb("Xs", [P, NBP, D], F32)
        Hs = sb("Hs", [P, NBP, D], F32)
        idx = [sb(f"idx{k}", [P, CH, T], I32) for k in range(2)]
        plan = [sb(f"planrow{k}", [1, 3, NG], I32) for k in range(2)]
        base = [sb(f"base{k}", [P, NG], I16) for k in range(2)]
        iof = sb("iof", [P, P], F32)
        iob = sb("iob", [P, P], BF16)
        iop = sb("iop", [P, 1], F32)
        iop16 = sb("iop16", [P, 1], I16)
        iof16 = sb("iof16", [P, P], I16)
        ident = sb("ident", [P, P], F32)
        bigI = sb("bigI", [P, P], BF16)
        onesb = sb("onesb", [P, P], BF16)
        onesf = sb("onesf", [1, P], F32)
        tri = sb("tri", [P, P], BF16)
        sel = sb("sel", [T * HEADS, T * HEADS, P], BF16)
        eps = sb("eps", [P, 1], F32)

        def chained(eng, name, c):
            s, n = sem(name, c), [0]

            def link(ins):
                n[0] += 1
                ins.then_inc(s, 1)
                eng.wait_ge(s, n[0])
            return link

        with Scope() as c:
            ioi = sb("ioi", [P, P], I32, c)
            iopi = sb("iopi", [P, 1], I32, c)
            empty = sb("empty", [P, RW], I32, c)
            s_io, s_x0, s_x, s_e, s_rec = (sem(n, c) for n in ("s_io", "s_x0", "s_x", "s_e", "s_rec"))
            s_c = sem("s_c", c)
            with nc.Block() as block:
                @block.gpsimd
                def _(pool):
                    pool.iota(ioi[:, :], pattern=[[1, P]], base=0, channel_multiplier=0).then_inc(s_io, 1)
                    pool.iota(iopi[:, :], pattern=[[0, 1]], base=0, channel_multiplier=1).then_inc(s_io, 1)

                @block.vector
                def _(dve):
                    link = chained(dve, "chain_c", c)
                    link(dve.memset(empty[:, :], 0))
                    ids = empty[:, :].rearrange("p (s w) -> p s w", w=RW)[:, :, 0:2]
                    dve.memset(ids, -1).then_inc(s_e, 1)
                    dve.memset(Xs[:, :, :], 0.0).then_inc(s_x0, 1)
                    dve.memset(onesb[:, :], 1.0)
                    dve.memset(onesf[:, :], 1.0)
                    dve.memset(eps[:, :], 1e-5)
                    dve.wait_ge(s_io, 2)
                    dve.tensor_copy(iof[:, :], ioi[:, :])
                    dve.tensor_copy(iob[:, :], ioi[:, :])
                    dve.tensor_copy(iop16[:, :], iopi[:, :])
                    dve.tensor_copy(iof16[:, :], ioi[:, :])
                    link(dve.tensor_copy(iop[:, :], iopi[:, :]))
                    dve.tensor_scalar(ident[:, :], iof[:, :], iop[:, 0:1], None, ALU.is_equal)
                    dve.tensor_scalar(bigI[:, :], iof[:, :], iop[:, 0:1], BIG, ALU.is_equal, ALU.mult)
                    dve.tensor_scalar(tri[:, :], iof[:, :], iop[:, 0:1], None, ALU.is_gt)
                    link(dve.tensor_scalar(sel[:, :, :], iof[0:T * HEADS, 0:T * HEADS].unsqueeze(2).to_broadcast([T * HEADS, T * HEADS, P]),
                                           iop[0:T * HEADS, 0:1], None, ALU.is_equal))

                @block.sync
                def _(sp):
                    sp.wait_ge(s_x0, 1)
                    sp.dma_start(Xs[:, 0:FULL, :], x[0:FULL * P, :].rearrange("(b p) f -> p b f", p=P)).then_inc(s_x, 16)
                    sp.dma_start(Xs[0:N - FULL * P, FULL, :], x[FULL * P:N, :]).then_inc(s_x, 16)
                    sp.wait_ge(s_e, 1)
                    parts = [(k, at) for k in range(2) for at in range(E, ER, P)]
                    for k, at in parts:
                        n = min(P, ER - at)
                        sp.dma_start(rec[k][at:at + n, :], empty[0:n, :]).then_inc(s_rec, 16)
                    sp.wait_ge(s_x, 32)
                    sp.wait_ge(s_rec, len(parts) * 16)

        with Scope() as c:
            ids = [sb(f"ids{k}", [EP, EC], I32, c) for k in range(2)]
            hi32 = sb("hi32", [EP, EC], I32, c)
            hi = [sb(f"hi{k}", [EP, EC], BF16, c) for k in range(2)]
            ohz = [[sb(f"oh{k}{u}", [P, 2 * CB - 1, NB], BF16, c) for u in range(U)] for k in range(2)]
            oh = [[t[:, CB - 1:, :] for t in ts] for ts in ohz]
            cnt = sb("cnt", [P, NB], F32, c)
            cnti = sb("cnti", [P, NB], I32, c)
            padded = sb("padded", [P, NB], F32, c)
            ends = sb("ends", [P, NB], F32, c)
            ones98 = sb("ones98", [P, NB], F32, c)
            gi = sb("gi", [GP, GQ], I32, c)
            gf = sb("gf", [GP, GQ], F32, c)
            past = sb("past", [GP, GQ, NB], F32, c)
            gb = sb("gb", [GP, GQ], F32, c)
            gbi = [sb(f"gbi{k}", [GP, 3, GQ], I32, c) for k in range(2)]
            start = sb("start", [GP, GQ], F32, c)
            before = sb("before", [P, NB], F32, c)
            base32 = [sb(f"base32{k}", [P, NG], I32, c) for k in range(2)]
            run = [sb(f"run{k}", [P, NB], F32, c) for k in range(2)]
            recs = [sb(f"recs{u}", [EP, CB, RW + 1], I32, c) for u in range(U)]
            val = [sb(f"val{k}", [EP, CB, NB], F32, c) for k in range(2)]
            pos = [sb(f"pos{k}", [EP, CB], F32, c) for k in range(2)]
            posi = [sb(f"posi{u}", [EP, CB], I32, c) for u in range(U)]
            s_ids, s_hi, s_oh, s_hist, s_histd = (sem(n, c) for n in ("s_ids", "s_hi", "s_oh", "s_hist", "s_histd"))
            s_gi, s_gbi, s_blk, s_start = (sem(n, c) for n in ("s_gi", "s_gbi", "s_blk", "s_start"))
            NC = EC // CB

            with nc.Block() as block:
                @block.sync
                def _(sp):
                    for k, a in enumerate((dst, src)):
                        sp.dma_start(ids[k][:, :], a.rearrange("(p c) -> p c", p=EP)).then_inc(s_ids, 16)
                    sp.wait_ge(s_gbi, 2)
                    for k in range(2):
                        sp.dma_start(plan_d[k].rearrange("a (p q) -> p a q", p=GP), gbi[k][:, :, :]).then_inc(s_blk, 16)
                    sp.wait_ge(s_blk, 32)
                    for k in range(2):
                        sp.dma_start(plan[k][:, :, :], plan_d[k].unsqueeze(0)).then_inc(s_blk, 16)
                        sp.dma_start(base32[k][:, :], plan_d[k][0:1, :].to_broadcast([P, NG])).then_inc(s_blk, 16)
                    sp.wait_ge(s_blk, 96)

                @block.gpsimd
                def _(pool):
                    pool.iota(gi[:, :], pattern=[[1, GQ]], base=0, channel_multiplier=GQ).then_inc(s_gi, 1)

                @block.vector
                def _(dve):
                    link = chained(dve, "chain_h", c)
                    for k in range(2):
                        for u in range(U):
                            dve.memset(ohz[k][u][:, 0:CB - 1, :], 0.0)
                    dve.wait_ge(s_ids, 32)
                    for k in range(2):
                        link(dve.tensor_scalar(hi32[:, :], ids[k][:, :], 7, None, ALU.arith_shift_right))
                        link(dve.tensor_copy(hi[k][:, :], hi32[:, :]))
                    for step in group_steps(dve, NC, 2, 0):
                        at = step(0)
                        if not at.first:
                            dve.wait_ge(s_hist, at.g - 1)
                        for k in range(2):
                            ins = dve.tensor_tensor(oh[k][at.slot][0:EP, :, :],
                                                    hi[k][:, ds(at.g * CB, CB)].unsqueeze(2).to_broadcast([EP, CB, NB]),
                                                    iob[0:EP, 0:NB].unsqueeze(1).to_broadcast([EP, CB, NB]), ALU.is_equal)
                        ins.then_inc(s_oh, 1)
                    dve.wait_ge(s_histd, 1)
                    dve.wait_ge(s_gi, 1)
                    link(dve.tensor_copy(gf[:, :], gi[:, :]))
                    link(dve.memset(ones98[:, :], 1.0))
                    for k in range(2):
                        link(dve.tensor_reduce(cnt[:, :], psum[k][:, 0:CB * NB].rearrange("p (c b) -> p b c", c=CB), X, ALU.add))
                        link(dve.tensor_tensor_scan(ends[:, :], ones98[:, :], cnt[:, :], 0.0, ALU.mult, ALU.add))
                        link(dve.tensor_tensor(run[k][:, :], ends[:, :], cnt[:, :], ALU.subtract))
                        link(dve.tensor_scalar(cnti[:, :], cnt[:, :], float(GE - 1), None, ALU.add))
                        link(dve.tensor_scalar(cnti[:, :], cnti[:, :], -GE, None, ALU.bitwise_and))
                        link(dve.tensor_copy(padded[:, :], cnti[:, :]))
                        link(dve.tensor_tensor_scan(ends[:, :], ones98[:, :], padded[:, :], 0.0, ALU.mult, ALU.add))
                        link(dve.tensor_tensor(before[:, :], ends[:, :], padded[:, :], ALU.subtract))
                        link(dve.tensor_tensor(before[:, :], run[k][:, :], before[:, :], ALU.subtract))
                        link(dve.tensor_scalar(ends[:, :], ends[:, :], 1.0 / GE, None, ALU.mult))
                        link(dve.tensor_tensor(past[:, :, :], gf[:, :].unsqueeze(2).to_broadcast([GP, GQ, NB]),
                                               ends[0:GP, :].unsqueeze(1).to_broadcast([GP, GQ, NB]), ALU.is_ge))
                        link(dve.tensor_reduce(gb[:, :], past[:, :, :], X, ALU.add))
                        link(dve.tensor_scalar(gb[:, :], gb[:, :], float(NB - 1), None, ALU.min))
                        link(dve.tensor_copy(gbi[k][:, 0, :], gb[:, :]))
                        link(dve.tensor_tensor(past[:, :, :], gb[:, :].unsqueeze(2).to_broadcast([GP, GQ, NB]),
                                               iof[0:GP, 0:NB].unsqueeze(1).to_broadcast([GP, GQ, NB]), ALU.is_equal))
                        link(dve.tensor_tensor(past[:, :, :], past[:, :, :], before[0:GP, :].unsqueeze(1).to_broadcast([GP, GQ, NB]), ALU.mult))
                        link(dve.tensor_reduce(start[:, :], past[:, :, :], X, ALU.add))
                        link(dve.scalar_tensor_tensor(start[:, :], gf[:, :], float(GE), start[:, :], ALU.mult, ALU.add))
                        link(dve.tensor_scalar(start[:, :], start[:, :], float(E), None, ALU.min))
                        link(dve.tensor_copy(gbi[k][:, 1, :], start[:, :]))
                        link(dve.tensor_scalar(gbi[k][:, 2, :], start[:, :], float(2 * GE - 1), None, ALU.add))
                        dve.tensor_scalar(gbi[k][:, 2, :], gbi[k][:, 2, :], GE.bit_length() - 1, None, ALU.arith_shift_right)\
                           .then_inc(s_gbi, 1)
                    dve.wait_ge(s_blk, 96)
                    for k in range(2):
                        dve.tensor_scalar(base[k][:, :], base32[k][:, :], float(P), None, ALU.mult)

                @block.tensor
                def _(pe):
                    for step in group_steps(pe, NC, 2, 0):
                        at = step(0)
                        pe.wait_ge(s_oh, at.g + 1)
                        for k in range(2):
                            ins = pe.matmul(psum[k][:, 0:CB * NB], onesb[0:EP, :],
                                            oh[k][at.slot][0:EP, :, :].rearrange("p c b -> p (c b)"),
                                            start=at.first and at.slot == 0, stop=False, skip_group_check=True)
                        ins.then_inc(s_hist, 1)
                    pe.wait_ge(s_hist, NC)
                    pe.nop().then_inc(s_histd, 1)

            s_oh2, s_rk, s_val, s_pos, s_ids2, s_nxt = (sem(n, c) for n in ("s_oh2", "s_rk", "s_val", "s_pos", "s_ids2", "s_nxt"))
            s_ea = [sem(f"s_ea{u}", c) for u in range(U)]
            s_slot = sem("s_slot", c)
            s_plain = [sem(f"s_plain{u}", c) for u in range(U)]
            s_sc = pool_dma
            ea_v = edge_attr.bitcast(I32).rearrange("(p c) f -> p c f", p=EP)

            with nc.Block() as block:
                @block.sync
                def _(sp):
                    plain_v = plain.rearrange("(p c) w -> p c w", p=EP)
                    for step in group_steps(sp, NC, U, 3):
                        if at := step(0):
                            if not at.first:
                                sp.wait_ge(s_sc[at.slot], at.turn * (16 * CB))
                                sp.sem_inc(s_slot, 1)
                                sp.wait_ge(s_plain[at.slot], at.turn * 16)
                            sp.dma_start(recs[at.slot][:, :, 2:RW], ea_v[:, ds(at.g * CB, CB), :]).then_inc(s_ea[at.slot], 16)
                        if at := step(3):
                            sp.wait_ge(s_ea[at.slot], (at.turn + 1) * 16)
                            sp.sem_inc(s_slot, 1)
                            sp.wait_ge(s_pos, at.g + 1)
                            sp.dma_start(plain_v[:, ds(at.g * CB, CB), :], recs[at.slot][:, :, :]).then_inc(s_plain[at.slot], 16)
                    for u in range(U):
                        sp.wait_ge(s_plain[u], NC // U * 16)

                @block.gpsimd
                def _(pool):
                    for step in group_steps(pool, NC, U, 0):
                        at = step(0)
                        pool.wait_ge(s_ea[at.slot], (at.turn + 1) * 16)
                        pool.wait_ge(s_pos, at.g + 1)
                        pool.sem_inc(s_start, 1)
                        for j in range(CB):
                            pool.indirect_dma_start(rec[0], bass.IndirectOffsetOnAxis(ap=posi[at.slot][:, j:j + 1], axis=0),
                                                    recs[at.slot][:, j, 0:RW], None).then_inc(s_sc[at.slot], 16)
                    for u in range(U):
                        pool.wait_ge(s_sc[u], NC // U * 16 * CB)
                        pool_base[u] = NC // U * 16 * CB

                @block.tensor
                def _(pe):
                    for step in group_steps(pe, NC, U, 0):
                        at = step(0)
                        pe.wait_ge(s_oh2, at.g + 1)
                        if not (at.first and at.slot < 2):
                            pe.wait_ge(s_pos, at.g - 1)
                        for k in range(2):
                            o = oh[k][at.slot]
                            for j in range(CB):
                                pe.matmul(psum[2 * k + at.slot % 2][:, 0:CB * NB], (onesb if j else tri)[0:EP, 0:P],
                                          ohz[k][at.slot][0:EP, CB - 1 - j:2 * CB - 1 - j, :].rearrange("p c b -> p (c b)"),
                                          start=j == 0, stop=j == CB - 1)
                            for j in range(CB):
                                ins = pe.matmul(psum[4 + 2 * k + at.slot % 2][:, 0:NB], onesb[0:EP, 0:P], o[0:EP, j, :],
                                                start=j == 0, stop=j == CB - 1)
                        ins.then_inc(s_rk, 1)

                @block.vector
                def _(dve):
                    for step in group_steps(dve, NC, U, 1):
                        at = step(0)
                        if at:
                            if not at.first:
                                dve.wait_ge(s_sc[at.slot], at.turn * (16 * CB))
                                dve.wait_ge(s_plain[at.slot], at.turn * 16)
                            for k in range(2):
                                dve.tensor_tensor(oh[k][at.slot][0:EP, :, :],
                                                  hi[k][:, ds(at.g * CB, CB)].unsqueeze(2).to_broadcast([EP, CB, NB]),
                                                  iob[0:EP, 0:NB].unsqueeze(1).to_broadcast([EP, CB, NB]),
                                                  ALU.is_equal).then_inc(s_oh2 if k else s_ids2, 1)
                            ri = recs[at.slot]
                            for k in range(2):
                                ins = dve.tensor_copy(ri[:, :, 1 - k:2 - k], ids[k][:, ds(at.g * CB, CB)].unsqueeze(2))
                        at = step(1)
                        if at:
                            dve.wait_ge(s_rk, at.g + 1)
                            dve.wait_ge(s_oh2, at.g + 1)
                            if not (isinstance(at.g, int) and at.g == 0):
                                dve.wait_ge(s_nxt, at.g * 2)
                            for k in range(2):
                                dve.tensor_tensor(val[k][:, :, :], psum[2 * k + at.slot % 2][0:EP, 0:CB * NB].rearrange("p (c b) -> p c b", c=CB),
                                                  run[k][0:EP, :].unsqueeze(1).to_broadcast([EP, CB, NB]), ALU.add).then_inc(s_val, 1)
                            for k in range(2):
                                dve.wait_ge(s_val, at.g * 6 + 1 + k)
                                dve.tensor_tensor(val[k][:, :, :], val[k][:, :, :], oh[k][at.slot][0:EP, :, :], ALU.mult).then_inc(s_val, 1)
                            for k in range(2):
                                dve.tensor_tensor(run[k][:, :], run[k][:, :], psum[4 + 2 * k + at.slot % 2][:, 0:NB], ALU.add).then_inc(s_nxt, 1)
                            for k in range(2):
                                dve.wait_ge(s_val, at.g * 6 + 3 + k)
                                dve.tensor_reduce(pos[k][:, :], val[k][:, :, :], X, ALU.add).then_inc(s_val, 1)
                            for k in range(2):
                                dve.wait_ge(s_val, at.g * 6 + 5 + k)
                                to = recs[at.slot][:, :, RW:RW + 1] if k else posi[at.slot][:, :].unsqueeze(2)
                                ins = dve.tensor_copy(to, pos[k][:, :].unsqueeze(2))
                            ins.then_inc(s_pos, 1)


        def read_back(k):
            with Scope() as c:
                back = [sb(f"back{u}", [P, CG, T, RW], I32, c) for u in range(2)]
                near = sb("near", [P, T, CH], F32, c)
                line = sb("line", [TR, CH // TR, P, T], I16, c)
                s_back = [sem(f"s_back{u}", c) for u in range(2)]
                s_free, s_rt, s_line, s_lined = (sem(n, c) for n in ("s_free", "s_rt", "s_line", "s_lined"))
                HB, TN = CH // CG, CH // TR * T
                with nc.Block() as block:
                    @block.sync
                    def _(sp):
                        for a in range(HB):
                            if a >= 2:
                                sp.wait_ge(s_free, a - 1)
                            sp.dma_start(back[a % 2].rearrange("p g j w -> p g (j w)"),
                                         rec[k].rearrange("(g p j) w -> p g (j w)", p=P, j=T)[:, a * CG:(a + 1) * CG, :])\
                              .then_inc(s_back[a % 2], 16)
                        sp.wait_ge(s_line, TN)
                        sp.dma_start(keys[k].rearrange("(b r e) -> r b e", r=TR, e=GE),
                                     line[:, :, :, :].rearrange("r b p j -> r b (p j)")).then_inc(s_lined, 16)
                        sp.wait_ge(s_lined, 16)

                    @block.vector
                    def _(dve):
                        for a in range(HB):
                            dve.wait_ge(s_back[a % 2], (a // 2 + 1) * 16)
                            at = slice(a * CG, (a + 1) * CG)
                            dve.tensor_scalar(idx[k][:, at, :], back[a % 2][:, :, :, k], 0.0, None, ALU.max)
                            dve.tensor_copy(near[:, :, at].rearrange("p j g -> p g j"), back[a % 2][:, :, :, 1 - k]).then_inc(s_free, 1)

                    @block.tensor
                    def _(pe):
                        pe.wait_ge(s_free, HB)
                        for n in range(TN):
                            if n >= 8:
                                pe.wait_ge(s_line, n - 7)
                            b, j = divmod(n, T)
                            pe.transpose(psum[n % 8][0:TR, 0:P], near[:, j, b * TR:(b + 1) * TR], ident[:, :]).then_inc(s_rt, 1)

                    @block.scalar
                    def _(act):
                        for n in range(TN):
                            b, j = divmod(n, T)
                            act.wait_ge(s_rt, n + 1)
                            act.activation(line[:, b, :, j], psum[n % 8][0:TR, 0:P], ACT.Copy).then_inc(s_line, 1)
        read_back(0)

        def normalise(c):
            mean = sb("mean", [P, NBP], F32, c)
            var = sb("var", [P, NBP], F32, c)
            dev = sb("dev", [P, NBP], F32, c)
            sq = sb("sq", [P, NBP, D], F32, c)
            s_var, s_sd = sem("s_var", c), sem("s_sd", c)
            wide3 = [P, NBP, D]
            with nc.Block() as block:
                @block.vector
                def _(dve):
                    link = chained(dve, "chain_n", c)
                    link(dve.tensor_reduce(mean[:, :], Xs[:, :, :], X, ALU.add))
                    link(dve.tensor_scalar(mean[:, :], mean[:, :], 1.0 / D, None, ALU.mult))
                    link(dve.tensor_tensor(Hs[:, :, :], Xs[:, :, :], mean[:, :].unsqueeze(2).to_broadcast(wide3), ALU.subtract))
                    link(dve.tensor_tensor(sq[:, :, :], Hs[:, :, :], Hs[:, :, :], ALU.mult))
                    dve.tensor_reduce(var[:, :], sq[:, :, :], X, ALU.add).then_inc(s_var, 1)
                    dve.wait_ge(s_sd, 1)
                    link(dve.reciprocal(mean[:, :], dev[:, :]))
                    link(dve.tensor_tensor(Hs[:, :, :], Hs[:, :, :], mean[:, :].unsqueeze(2).to_broadcast(wide3), ALU.mult))
                    dve.tensor_scalar(Hs[:, :, :], Hs[:, :, :], 0.0, None, ALU.max)

                @block.scalar
                def _(act):
                    act.wait_ge(s_var, 1)
                    act.activation(dev[:, :], var[:, :], ACT.Sqrt, bias=eps[:, 0:1], scale=1.0 / D).then_inc(s_sd, 1)

        def node_rows(table, row):
            return table.rearrange("(b p) w -> p b w", p=P)

        def store(pairs, c, name):
            s = sem(name, c)
            with nc.Block() as block:
                @block.sync
                def _(sp):
                    for to, of in pairs:
                        sp.dma_start(to.rearrange("(b p) w -> p b w", p=P), of).then_inc(s, 16)
                    sp.wait_ge(s, 16 * len(pairs))

        def diagonal(c, name, weights, R, width, rows=None):
            rows = rows or P // R
            t = sb(name, [P, R * width], F32, c)
            s0, s1 = sem(name + "_0", c), sem(name + "_1", c)
            with nc.Block() as block:
                @block.vector
                def _(dve):
                    dve.memset(t[:, :], 0.0).then_inc(s0, 1)

                @block.sync
                def _(sp):
                    sp.wait_ge(s0, 1)
                    for r in range(R):
                        for at, w in weights:
                            sp.dma_start(t[r * rows:(r + 1) * rows, r * width + at:r * width + at + w.shape[1]], w).then_inc(s1, 16)
                    sp.wait_ge(s1, R * len(weights) * 16)
            return t

        def bias_rows(c, name, items, width, R):
            t = sb(name, [1, R, width], F32, c)
            s1 = sem(name + "_1", c)
            with nc.Block() as block:
                @block.sync
                def _(sp):
                    for r in range(R):
                        for at, w in items:
                            sp.dma_start(t[0:1, r, at:at + w.shape[0]], w.unsqueeze(0)).then_inc(s1, 16)
                    sp.wait_ge(s1, R * len(items) * 16)
            return t[:, :, :].rearrange("a r w -> a (r w)")

        def node_matmul(name, c, steps, take, weights, bias, put, hidden=None):
            W = weights.shape[1]
            part = [sb(f"part{u}", [P, P], F32, c) for u in range(2)]
            turned = [sb(f"turned{u}", [P, P], F32, c) for u in range(2)]
            hid = [sb(f"hid{u}", [P, P], F32, c) for u in range(2)] if hidden else turned
            s_part, s_tr, s_in, s_h, s_hr, s_mm, s_out = (sem(name + n, c) for n in ("part", "tr", "in", "h", "hr", "mm", "out"))
            with nc.Block() as block:
                @block.vector
                def _(dve):
                    for step in group_steps(dve, steps, 2, 2):
                        at = step(0)
                        if at:
                            if not at.first:
                                dve.wait_ge(s_tr, at.g - 1)
                            take(dve, at.g, part[at.slot]).then_inc(s_part, 1)
                        at = step(2)
                        if at:
                            dve.wait_ge(s_mm, at.g + 1)
                            put(dve, at.g, psum[4 + at.slot][:, 0:W]).then_inc(s_out, 1)

                @block.scalar
                def _(act):
                    for step in group_steps(act, steps, 2, 1):
                        at = step(0)
                        if at:
                            if not at.first:
                                act.wait_ge(s_h if hidden else s_mm, at.g - 1)
                            act.wait_ge(s_tr, at.g + 1)
                            act.activation(turned[at.slot][:, :], psum[at.slot][:, 0:P], ACT.Copy).then_inc(s_in, 1)
                        at = step(1)
                        if at and hidden:
                            if not at.first:
                                act.wait_ge(s_mm, at.g - 1)
                            act.wait_ge(s_h, at.g + 1)
                            act.activation(hid[at.slot][:, :], psum[2 + at.slot][:, 0:P], ACT.Relu, bias=hidden[1][:, 0:1]).then_inc(s_hr, 1)

                @block.tensor
                def _(pe):
                    for step in group_steps(pe, steps, 2, 1):
                        at = step(0)
                        if at:
                            if not at.first:
                                pe.wait_ge(s_in, at.g - 1)
                            pe.wait_ge(s_part, at.g + 1)
                            pe.transpose(psum[at.slot][:, 0:P], part[at.slot][:, :], ident[:, :]).then_inc(s_tr, 1)
                        at = step(1)
                        if at:
                            if hidden:
                                pe.wait_ge(s_in, at.g + 1)
                                if not at.first:
                                    pe.wait_ge(s_hr, at.g - 1)
                                pe.matmul(psum[2 + at.slot][:, 0:P], hidden[0][:, :], turned[at.slot][:, :], start=True, stop=True)\
                                  .then_inc(s_h, 1)
                            pe.wait_ge(s_hr if hidden else s_in, at.g + 1)
                            if not at.first:
                                pe.wait_ge(s_out, at.g - 1)
                            if bias is not None:
                                pe.matmul(psum[4 + at.slot][:, 0:W], onesf[:, :], bias, start=True, stop=False)
                            pe.matmul(psum[4 + at.slot][:, 0:W], hid[at.slot][:, :], weights, start=bias is None, stop=True)\
                              .then_inc(s_mm, 1)

        def three_parts(dve, link, parts, whole, rest):
            link(dve.tensor_copy(parts[0], whole))
            link(dve.tensor_tensor(rest, whole, parts[0], ALU.subtract))
            link(dve.tensor_copy(parts[1], rest))
            link(dve.tensor_tensor(rest, rest, parts[1], ALU.subtract))
            link(dve.tensor_copy(parts[2], rest))

        class Pass:

            def __init__(self, name, c, k, width, table, rows, local=None, feats=False, hot=BF16, beside=None):
                self.k, self.width, self.table, self.rows, self.local, self.feats = k, width, table, rows, local, feats
                self.hot_type, self.beside, dt = hot, beside, table.dtype
                self.sem = lambda n: sem(f"{name}_{n}", c)
                self.sb = lambda n, shape, dt: sb(f"{name}_{n}", shape, dt, c)
                self.ring = lambda n, shape, dt, depth=U: [sb(f"{name}_{n}{u}", shape, dt, c) for u in range(depth)]
                self.list = self.ring("list", [P, T], I32)
                self.got = self.ring("got", [P, T, width], dt)
                self.far = self.ring("far", [P, T, width + (DE if feats else 0)], dt)
                self.key = self.ring("key", [P, T], I16)
                self.oe = self.ring("oe", [P, T, P], hot)
                self.listed = [self.sem(f"listed{u}") for u in range(U)]
                self.written = [self.sem(f"written{u}") for u in range(U)]
                self.loaded = [self.sem(f"loaded{u}") for u in range(U)]
                self.hot, self.summed, self.done, self.go, self.keyed, self.there = (
                    self.sem(n) for n in ("hot", "summed", "done", "go", "keyed", "there"))
                self.base = list(pool_base)
                for u in range(U):
                    pool_base[u] += CH // U * T * 16
                self.loads = 2 + (2 if local is not None else 0) + feats
                if local is not None:
                    self.row = self.ring("row", [P, GE], I16)
                    self.ot = self.ring("ot", [P, P, T], BF16)
                    self.loc = self.ring("loc", [P, local.shape[1]], BF16)

            def ot_tile(self, at, j):
                return self.ot[at.slot][:, :, j]

            def ot_all(self, at):
                return self.ot[at.slot][:, :, :].rearrange("n p j -> n j p")

            def feed(self, sp):
                for step in group_steps(sp, CH, U, U, peel=2):
                    if at := step(0):
                        if not at.first:
                            sp.wait_ge(pool_dma[at.slot], at.turn * (16 * T) + self.base[at.slot])
                            sp.sem_inc(self.keyed, 1)
                        sp.dma_start(self.list[at.slot][:, :], idx[self.k][:, ds(at.g, 1), :].rearrange("p a j -> p (a j)"))\
                          .then_inc(self.listed[at.slot], 16)
                        if self.beside:
                            self.beside.fetch(sp, at)
                    if at := step(3):
                        sp.wait_ge(pool_dma[at.slot], (at.turn + 1) * (16 * T) + self.base[at.slot])
                        sp.dma_start(self.rows[ds(at.g * GE, GE), :].rearrange("(p j) w -> p (j w)", j=T),
                                     self.got[at.slot][:, :, :].rearrange("p j w -> p (j w)")).then_inc(self.written[at.slot], 16)
                    if at := step(5):
                        sp.wait_ge(self.written[at.slot], (at.turn + 1) * 16)
                        sp.sem_inc(self.there, 1)
                    if at := step(U):
                        self.load_keys(sp, at)
                if self.beside:
                    for n in range(RF):
                        self.beside.fetch_rest(sp, n, n % RR, n // RR)
                with sp.Fori(0, (NG - CH) // U) as i:
                    for u in range(U):
                        self.load_keys(sp, At(i * U + (CH + u), u, i + CH // U))
                        if self.beside and u < RR:
                            n = RF + u
                            self.beside.fetch_rest(sp, i * RR + n, n % RR, i + n // RR)

            def load_keys(self, sp, at):
                u, row = at.slot, plan[self.k]
                start = sp.value_load(row[0:1, 1, ds(at.g, 1)], min_val=0, max_val=E)
                if self.local is not None:
                    b = sp.value_load(row[0:1, 0, ds(at.g, 1)], min_val=0, max_val=NB - 1)
                if not at.first:
                    sp.wait_ge(self.done, at.g - (U - 1))
                    sp.sem_inc(self.keyed, 1)
                edges = ds(start, GE)
                sp.dma_start(self.key[u][:, :], keys[self.k][edges].rearrange("(p j) -> p j", j=T)).then_inc(self.loaded[u], 16)
                if self.local is not None:
                    sp.dma_start(self.row[u][:, :], keys[self.k][edges].unsqueeze(0).to_broadcast([P, GE])).then_inc(self.loaded[u], 16)
                    sp.dma_start(self.loc[u][:, :], self.local[ds(b * P, P), :]).then_inc(self.loaded[u], 16)

            def gather(self, pool):
                for step in group_steps(pool, CH, U, 0):
                    at = step(0)
                    pool.wait_ge(self.listed[at.slot], (at.turn + 1) * 16)
                    if not at.first:
                        pool.wait_ge(self.there, at.g - (U - 1))
                    pool.sem_inc(self.go, 1)
                    for j in range(T):
                        pool.indirect_dma_start(self.got[at.slot][:, j, :], None, self.table,
                                                bass.IndirectOffsetOnAxis(ap=self.list[at.slot][:, j:j + 1], axis=0))\
                            .then_inc(pool_dma[at.slot], 16)
                    if self.beside:
                        self.beside.put(pool, at)
                if self.beside:
                    self.beside.put_rest(pool)

            def load(self, act, at):
                u, row = at.slot, plan[self.k]
                start = act.value_load(row[0:1, 1, ds(at.g, 1)], min_val=0, max_val=E)
                need = act.value_load(row[0:1, 2, ds(at.g, 1)], min_val=1, max_val=CH)
                if not at.first:
                    act.wait_ge(self.done, at.g - (U - 1))
                act.wait_ge(self.there, need)
                act.sem_inc(self.go, 1)
                edges = ds(start, GE)
                rows = self.rows[edges, :].rearrange("(p j) w -> p j w", j=T)
                if self.feats:
                    act.dma_start(self.far[u][:, :, 0:self.width], rows).then_inc(self.loaded[u], 16)
                    act.dma_start(self.far[u][:, :, self.width:], rec[self.k].bitcast(F32)[edges, 2:RW].rearrange("(p j) w -> p j w", j=T))\
                       .then_inc(self.loaded[u], 16)
                else:
                    act.dma_start(self.far[u][:, :, :].rearrange("p j w -> p (j w)"), rows.rearrange("p j w -> p (j w)"))\
                       .then_inc(self.loaded[u], 16)

            def here(self, at):
                return (at.turn + 1) * (16 * self.loads)

            def edges_hot(self, dve, at):
                u, first = at.slot, base[self.k][:, ds(at.g, 1)]
                dve.wait_ge(self.loaded[u], self.here(at))
                if self.local is not None:
                    dve.tensor_scalar(self.ot[u][:, :, :].rearrange("n p j -> n (p j)"), self.row[u][:, :], iop16[:, 0:1], first,
                                      ALU.subtract, ALU.is_equal)
                yield
                nodes = iof16 if self.hot_type == BF16 else iof
                for j in range(T):
                    ins = dve.tensor_scalar(self.oe[u][:, j, :], nodes[:, :], first, self.key[u][:, j:j + 1], ALU.add, ALU.is_equal)
                    if j == T - 1:
                        ins.then_inc(self.hot, 1)
                    yield

            def splitter(self, n):
                self.part = self.ring("part", [P, 3, n], BF16, 2)
                self.rest = self.sb("rest", [P, n], F32)
                self.split_done = self.sem("split_done")

            def split(self, dve, at, whole):
                part, g = self.part[at.slot % 2], at.g * 4
                if not (isinstance(at.g, int) and at.g < 2):
                    dve.wait_ge(self.summed, at.g - 1)
                dve.tensor_copy(part[:, 0, :], whole).then_inc(self.split_done, 1)
                yield
                dve.wait_ge(self.split_done, g + 1)
                dve.tensor_tensor(self.rest[:, :], whole, part[:, 0, :], ALU.subtract).then_inc(self.split_done, 1)
                yield
                dve.wait_ge(self.split_done, g + 2)
                dve.tensor_copy(part[:, 1, :], self.rest[:, :]).then_inc(self.split_done, 1)
                yield
                dve.wait_ge(self.split_done, g + 3)
                dve.tensor_tensor(part[:, 2, :], self.rest[:, :], part[:, 1, :], ALU.subtract).then_inc(self.split_done, 1)
                yield

            def split_at(self, at):
                return at.g * 4 + 4

            def segment_sum(self, pe, at, values, width, parts, ones=False):
                if not (isinstance(at.g, int) and at.g < 2):
                    pe.wait_ge(self.done, at.g - 1)
                bank = psum[6 + at.slot % 2]
                for j in range(T):
                    for i in range(parts):
                        ins = pe.matmul(bank[:, 0:width], self.oe[at.slot][:, j, :], values(j, i),
                                        start=j + i == 0, stop=j == T - 1 and i == parts - 1)
                if ones:
                    for j in range(T):
                        ins = pe.matmul(bank[:, width:width + 1], self.oe[at.slot][:, j, :], onesb[:, 0:1], start=j == 0, stop=j == T - 1)
                ins.then_inc(self.summed, 1)

            def block_of(self, eng, at):
                return eng.value_load(plan[self.k][0:1, 0, ds(at.g, 1)], min_val=0, max_val=NB - 1)

            def add(self, dve, at, acc, width):
                dve.wait_ge(self.summed, at.g + 1)
                if not (isinstance(at.g, int) and at.g == 0):
                    dve.wait_ge(self.done, at.g)
                b = self.block_of(dve, at)
                mine = acc[:, ds(b, 1), :].rearrange("p a w -> p (a w)")
                dve.tensor_tensor(mine, mine, psum[6 + at.slot % 2][:, 0:width], ALU.add).then_inc(self.done, 1)

        class SecondOrder:

            def __init__(self, c):
                self.record = [sb(f"record{u}", [EP, CR, RW + 1], I32, c) for u in range(U)]
                self.fetched = [sem(f"fetched{u}", c) for u in range(U)]
                self.go = sem("put_go", c)
                self.columns = plain.rearrange("(p c) w -> p c w", p=EP)

            def fetch(self, sp, at):
                if not at.first:
                    sp.wait_ge(pool_put[at.slot], at.turn * (16 * CS))
                sp.dma_start(self.record[at.slot][:, 0:CS, :], self.columns[:, ds(at.g * CS, CS), :]).then_inc(self.fetched[at.slot], 16)

            def fetch_rest(self, sp, n, slot, turn):
                sp.wait_ge(pool_put[slot], turn * (16 * CR) + CH // U * 16 * CS)
                sp.dma_start(self.record[slot][:, :, :], self.columns[:, ds(n * CR + CH * CS, CR), :]).then_inc(self.fetched[slot], 16)

            def scatter(self, pool, slot, columns):
                pool.sem_inc(self.go, 1)
                for j in range(columns):
                    pool.indirect_dma_start(rec[1], bass.IndirectOffsetOnAxis(ap=self.record[slot][:, j, RW:RW + 1], axis=0),
                                            self.record[slot][:, j, 0:RW], None).then_inc(pool_put[slot], 16)

            def put(self, pool, at):
                pool.wait_ge(self.fetched[at.slot], (at.turn + 1) * 16)
                self.scatter(pool, at.slot, CS)

            def put_rest(self, pool):
                with pool.Fori(0, RS // RR) as i:
                    for slot in range(RR):
                        pool.wait_ge(self.fetched[slot], i * 16 + (CH // U + 1) * 16)
                        self.scatter(pool, slot, CR)
                for n in range(RS // RR * RR, RS):
                    pool.wait_ge(self.fetched[n % RR], (CH // U + n // RR + 1) * 16)
                    self.scatter(pool, n % RR, CR)
                for u in range(U):
                    rest = (RS - u + RR - 1) // RR if u < RR else 0
                    pool.wait_ge(pool_put[u], CH // U * (16 * CS) + rest * (16 * CR))

        with Scope() as c:
            normalise(c)
            acc = sb("acc0", [P, NBP, D + 1], F32, c)
            hs3 = sb("hs3", [P, NBP, 3, D], BF16, c)
            rest0 = sb("rest0", [P, NBP, D], F32, c)
            with nc.Block() as block:
                @block.vector
                def _(dve):
                    three_parts(dve, chained(dve, "chain_00", c), [hs3[:, :, i, :] for i in range(3)], Hs[:, :, :], rest0[:, :, :])
            store([(gath[0], hs3[:, :, :, :].rearrange("p b i w -> p b (i w)"))], c, "st0")
            ps = Pass("l0", c, 0, 3 * D, gath[0], rows[0])
            s_acc0 = sem("s_acc0", c)
            with nc.Block() as block:
                @block.sync
                def _(sp):
                    ps.feed(sp)

                @block.gpsimd
                def _(pool):
                    ps.gather(pool)

                @block.scalar
                def _(act):
                    for step in group_steps(act, NG, U, 0):
                        ps.load(act, step(0))

                @block.tensor
                def _(pe):
                    for step in group_steps(pe, NG, U, 0):
                        at = step(0)
                        pe.wait_ge(ps.hot, at.g + 1)
                        ps.segment_sum(pe, at, lambda j, i: ps.far[at.slot][:, j, i * D:(i + 1) * D], D, 3, ones=True)

                @block.vector
                def _(dve):
                    dve.memset(acc[:, :, :], 0.0).then_inc(s_acc0, 1)
                    dve.wait_ge(s_acc0, 1)
                    for step in group_steps(dve, NG, U, 1):
                        if at := step(0):
                            list(ps.edges_hot(dve, at))
                        if at := step(1):
                            ps.add(dve, at, acc, D + 1)

            both = sb("both0", [P, NBP, 2 * D], F32, c)
            count = sb("count", [P, NBP], F32, c)
            with nc.Block() as block:
                @block.vector
                def _(dve):
                    link = chained(dve, "chain_0", c)
                    link(dve.tensor_scalar(count[:, :], acc[:, :, D], 1.0, None, ALU.max))
                    link(dve.reciprocal(count[:, :], count[:, :]))
                    dve.tensor_copy(both[:, :, 0:D], Hs[:, :, :])
                    dve.tensor_tensor(both[:, :, D:2 * D], acc[:, :, 0:D], count[:, :].unsqueeze(2).to_broadcast([P, NBP, D]), ALU.mult)
            w = diagonal(c, "w0", [(0, W0)], 2, D)
            bias = bias_rows(c, "bias0", [(0, b0)], D, 2)

            def put0(dve, i, value):
                mine = Xs[:, ds(i * 2, 2), :].rearrange("p r f -> p (r f)")
                return dve.scalar_tensor_tensor(mine, value, 0.0, mine, ALU.max, ALU.add)
            node_matmul("n0", c, NBP // 2, lambda dve, i, to: dve.tensor_copy(to[:, :].rearrange("p (r f) -> p r f", r=2), both[:, ds(i * 2, 2), :]),
                        w[:, :], bias, put0)

        def softmax_pass(name, c, k, width, table, rows, local, heads_w, acc, best, scores_in, scores, spread, parts, beside=None):
            ps = Pass(name, c, k, width, table, rows, local, hot=BF16 if parts == 3 else F32, beside=beside)
            W = HEADS * heads_w
            if parts == 3:
                ps.splitter(T * W)
            sc = ps.ring("sc", [P, T, HEADS], F32)
            turned = ps.ring("turned", [T * HEADS, P], BF16, 2)
            top = ps.sb("top", [P, HEADS], F32)
            new = ps.ring("new", [P, HEADS], BF16)
            fall = ps.ring("fall", [P, HEADS], F32)
            keep = ps.ring("keep", [P, HEADS], F32)
            less = ps.ring("less", [P, T, HEADS], F32)
            val = ps.ring("val", [P, T, HEADS, heads_w], F32, 2)
            (s_near, s_tmp, s_sc, s_turn, s_turned, s_cast, s_top, s_new, s_fall, s_best, s_keep, s_under, s_less, s_weight,
             s_val, s_kept, s_init) = (ps.sem(n) for n in (
                 "near", "tmp", "sc", "turn", "turned", "cast", "top", "new", "fall", "best", "keep", "under", "less", "weight",
                 "val", "kept", "init"))

            def under(at):
                return psum[0][:, 384:384 + T * HEADS]

            with nc.Block() as block:
                @block.sync
                def _(sp):
                    ps.feed(sp)

                @block.gpsimd
                def _(pool):
                    ps.gather(pool)

                @block.vector
                def _(dve):
                    dve.memset(best[:, :, :], -NONE).then_inc(s_init, 1)
                    dve.memset(acc[:, :, :], 0.0).then_inc(s_init, 1)
                    dve.wait_ge(s_init, 2)
                    for step in group_steps(dve, NG, U, 6):
                        hot = ps.edges_hot(dve, step(0)) if step(0) else iter(())
                        if at := step(4):
                            for i in range(2):
                                dve.wait_ge(s_cast, at.g * 2 + 1 + i)
                                dve.tensor_reduce(top[:, 2 * i:2 * i + 2], wide[:, 2 * i:2 * i + 2, :], X, ALU.max, negate=True)\
                                   .then_inc(s_top, 1)
                            b = ps.block_of(dve, at)
                            mine = best[:, ds(b, 1), :].rearrange("p a h -> p (a h)")
                            dve.wait_ge(s_top, at.g * 2 + 2)
                            if not (isinstance(at.g, int) and at.g == 0):
                                dve.wait_ge(s_best, at.g)
                            dve.scalar_tensor_tensor(new[at.slot][:, :], top[:, :], BIG, mine, ALU.add, ALU.min).then_inc(s_new, 1)
                            next(hot, None)
                            dve.wait_ge(s_new, at.g + 1)
                            dve.tensor_tensor(fall[at.slot][:, :], new[at.slot][:, :], mine, ALU.subtract).then_inc(s_fall, 1)
                            next(hot, None)
                            dve.wait_ge(s_fall, at.g + 1)
                            dve.tensor_scalar(mine, new[at.slot][:, :], -NONE, None, ALU.min).then_inc(s_best, 1)
                        list(hot)
                        if at := step(4):
                            dve.wait_ge(s_under, at.g + 1)
                            dve.tensor_tensor(less[at.slot][:, :, :], sc[at.slot][:, :, :], under(at).rearrange("p (j h) -> p j h", h=HEADS),
                                              ALU.add).then_inc(s_less, 1)
                        if at := step(2):
                            dve.wait_ge(s_near, at.g + 1)
                            score = scores(dve, at, ps.far, sc[at.slot], s_tmp, s_sc)
                            next(score)
                        if at := step(5):
                            dve.wait_ge(s_weight, at.g + 1)
                            spread(dve, ps.far[at.slot], val[at.slot % 2]).then_inc(s_val, 1)
                        if step(2):
                            next(score)
                        split = iter(())
                        if parts == 3 and (at := step(5)):
                            dve.wait_ge(s_val, at.g + 1)
                            split = ps.split(dve, at, val[at.slot % 2][:, :, :, :].rearrange("p j h w -> p (j h w)"))
                        next(split, None)
                        if at := step(6):
                            b = ps.block_of(dve, at)
                            mine = acc[:, ds(b, 1), :].rearrange("p a w -> p (a w)")
                            heads = mine.rearrange("p (h w) -> p h w", h=HEADS)
                            dve.wait_ge(s_keep, at.g + 1)
                            if not (isinstance(at.g, int) and at.g == 0):
                                dve.wait_ge(ps.done, at.g)
                            dve.tensor_tensor(heads, heads, keep[at.slot][:, :].unsqueeze(2).to_broadcast([P, HEADS, heads_w]),
                                              ALU.mult).then_inc(s_kept, 1)
                            next(split, None)
                            dve.wait_ge(ps.summed, at.g + 1)
                            dve.wait_ge(s_kept, at.g + 1)
                            dve.tensor_tensor(mine, mine, psum[6 + at.slot % 2][:, 0:W], ALU.add).then_inc(ps.done, 1)
                        list(split)

                @block.scalar
                def _(act):
                    for step in group_steps(act, NG, U, 6):
                        if at := step(6):
                            act.wait_ge(s_fall, at.g + 1)
                            act.activation(keep[at.slot][:, :], fall[at.slot][:, :], ACT.Exp).then_inc(s_keep, 1)
                        if at := step(4):
                            if not (isinstance(at.g, int) and at.g < 2):
                                act.wait_ge(s_cast, at.g * 2 - 2)
                            act.wait_ge(s_turn, at.g + 1)
                            act.activation(turned[at.slot % 2][:, :], psum[1][0:T * HEADS, 0:P], ACT.Copy).then_inc(s_turned, 1)
                        if at := step(6):
                            if not (isinstance(at.g, int) and at.g < 2):
                                act.wait_ge(ps.summed, at.g - 1)
                            act.wait_ge(s_less, at.g + 1)
                            act.activation(val[at.slot % 2][:, :, :, heads_w - 1], less[at.slot][:, :, :], ACT.Exp).then_inc(s_weight, 1)
                        if at := step(0):
                            ps.load(act, at)

                @block.tensor
                def _(pe):
                    def cast(at, i):
                        pe.wait_ge(s_turned, at.g + 1)
                        if not (isinstance(at.g, int) and at.g == 0):
                            pe.wait_ge(s_top, at.g * 2 - 1 + i)
                        for h in (2 * i, 2 * i + 1):
                            pe.matmul(wide[:, h, :], bigI[:, :], ps.ot_all(at), start=True, stop=False, skip_group_check=True)
                            for j in range(T):
                                ins = pe.matmul(wide[:, h, j * P:(j + 1) * P], sel[:, j * HEADS + h, :], turned[at.slot % 2][:, :],
                                                start=False, stop=True, skip_group_check=True)
                        ins.then_inc(s_cast, 1)

                    for step in group_steps(pe, NG, U, 5):
                        if at := step(3):
                            cast(at, 0)
                        if at := step(4):
                            pe.wait_ge(s_new, at.g + 1)
                            for j in range(T):
                                ins = pe.matmul(under(at)[:, j * HEADS:(j + 1) * HEADS], ps.ot_tile(at, j), new[at.slot][:, :],
                                                start=True, stop=True)
                            ins.then_inc(s_under, 1)
                        if at := step(3):
                            cast(at, 1)
                        if at := step(2):
                            pe.wait_ge(s_sc, at.g + 1)
                            if not (isinstance(at.g, int) and at.g == 0):
                                pe.wait_ge(s_turned, at.g)
                            pe.transpose(psum[1][0:T * HEADS, 0:P], sc[at.slot][:, :, :].rearrange("p j h -> p (j h)"), ident[:, :])\
                              .then_inc(s_turn, 1)
                        if at := step(1):
                            pe.wait_ge(ps.hot, at.g + 1)
                            if not (isinstance(at.g, int) and at.g == 0):
                                pe.wait_ge(s_sc, at.g)
                            scores_in(pe, at, ps).then_inc(s_near, 1)
                        if at := step(5):
                            if parts == 3:
                                pe.wait_ge(ps.split_done, ps.split_at(at))
                                ps.segment_sum(pe, at, lambda j, i: ps.part[at.slot % 2][:, i, j * W:(j + 1) * W], W, 3)
                            else:
                                pe.wait_ge(s_val, at.g + 1)
                                ps.segment_sum(pe, at, lambda j, i: val[at.slot % 2][:, j, :, :].rearrange("p h w -> p (h w)"), W, 1)

        def near_part(width):
            def run(pe, at, ps):
                for j in range(T):
                    for i in range(3):
                        ins = pe.matmul(psum[0][:, j * width:(j + 1) * width], ps.ot_tile(at, j),
                                        ps.loc[at.slot][:, i * width:(i + 1) * width], start=i == 0, stop=i == 2)
                return ins
            return run

        with Scope() as c:
            normalise(c)
            tab = sb("tab1", [P, NBP, 3 * D], F32, c)
            w = diagonal(c, "w1", [(0, Wq), (D, Wk), (2 * D, Wv)], 4, 3 * D)
            node_matmul("n1", c, NBP // 4, lambda dve, i, to: dve.tensor_copy(to[:, :].rearrange("p (r f) -> p r f", r=4), Hs[:, ds(i * 4, 4), :]),
                        w[:, :], None, lambda dve, i, value: dve.tensor_copy(tab[:, ds(i * 4, 4), :].rearrange("p r w -> p (r w)"), value))
            with Scope() as c2:
                qs = sb("qs", [P, NBP, 3, D], BF16, c2)
                rest = sb("rest", [P, NBP, D], F32, c2)
                with nc.Block() as block:
                    @block.vector
                    def _(dve):
                        link = chained(dve, "chain_1", c2)
                        q = tab[:, :, 0:D]
                        link(dve.tensor_scalar(q, q, DH ** -0.5, None, ALU.mult))
                        three_parts(dve, link, [qs[:, :, i, :] for i in range(3)], q, rest[:, :, :])
                store([(locl[1], qs[:, :, :, :].rearrange("p b i w -> p b (i w)")), (gath[1], tab[:, :, D:3 * D])], c2, "st1")

        with Scope() as c:
            acc = sb("acc1", [P, NBP, D + HEADS], F32, c)
            best = sb("best1", [P, NBP, HEADS], F32, c)
            with Scope() as c2:
                prod = [sb(f"prod{u}", [P, T, D], F32, c2) for u in range(2)]

                def score1(dve, at, far, sc, s_tmp, s_sc):
                    dve.tensor_tensor(prod[at.slot % 2][:, :, :], psum[0][:, 0:T * D].rearrange("p (j w) -> p j w", j=T), far[at.slot][:, :, 0:D],
                                      ALU.mult).then_inc(s_tmp, 1)
                    yield
                    dve.wait_ge(s_tmp, at.g + 1)
                    dve.tensor_reduce(sc[:, :, :], prod[at.slot % 2][:, :, :].rearrange("p j (h d) -> p j h d", d=DH), X, ALU.add).then_inc(s_sc, 1)
                    yield

                def spread1(dve, far, val):
                    return dve.tensor_tensor(val[:, :, :, 0:DH], far[:, :, D:2 * D].rearrange("p j (h d) -> p j h d", d=DH),
                                             val[:, :, :, DH:DH + 1].to_broadcast([P, T, HEADS, DH]), ALU.mult)
                softmax_pass("l1", c2, 0, 2 * D, gath[1], rows[1], locl[1], DH + 1, acc, best, near_part(D), score1, spread1, 3, SecondOrder(c2))
            att = sb("att1", [P, NBP, D], F32, c)
            den = sb("den1", [P, NBP, HEADS], F32, c)
            with nc.Block() as block:
                @block.vector
                def _(dve):
                    link = chained(dve, "chain_1b", c)
                    a4 = acc[:, :, :].rearrange("p b (h w) -> p b h w", h=HEADS)
                    link(dve.tensor_scalar(den[:, :, :], a4[:, :, :, DH], 1e-16, None, ALU.max))
                    link(dve.reciprocal(den[:, :, :], den[:, :, :]))
                    dve.tensor_tensor(att[:, :, :].rearrange("p b (h d) -> p b h d", h=HEADS), a4[:, :, :, 0:DH],
                                      den[:, :, :].unsqueeze(3).to_broadcast([P, NBP, HEADS, DH]), ALU.mult)
                    dve.tensor_tensor(Xs[:, :, :], Xs[:, :, :], Hs[:, :, :], ALU.add)
            w = diagonal(c, "wo", [(0, Wo)], 4, D)

            def add_rows(R):
                def put(dve, i, value):
                    mine = Xs[:, ds(i * R, R), :].rearrange("p r f -> p (r f)")
                    return dve.tensor_tensor(mine, mine, value, ALU.add)
                return put
            node_matmul("n1b", c, NBP // 4, lambda dve, i, to: dve.tensor_copy(to[:, :].rearrange("p (r f) -> p r f", r=4), att[:, ds(i * 4, 4), :]),
                        w[:, :], None, add_rows(4))

        read_back(1)

        with Scope() as c:
            normalise(c)
            tab = sb("tab2", [P, NBP, 2 * H2], F32, c)
            w = diagonal(c, "w2", [(0, W1f[0:D, :]), (H2, W1b[0:D, :])], 4, 2 * H2)
            bias = bias_rows(c, "bias2", [(0, b1f), (H2, b1b)], 2 * H2, 4)
            node_matmul("n2", c, NBP // 4, lambda dve, i, to: dve.tensor_copy(to[:, :].rearrange("p (r f) -> p r f", r=4), Hs[:, ds(i * 4, 4), :]),
                        w[:, :], bias, lambda dve, i, value: dve.tensor_copy(tab[:, ds(i * 4, 4), :].rearrange("p r w -> p (r w)"), value))
            store([(gath[2], Hs[:, :, :])], c, "st2")
            us = sb("us", [P, NBP, 3, H2], BF16, c)
            rest = sb("rest2", [P, NBP, H2], F32, c)
            for way, to in ((0, locl[2]), (1, locl[4])):
                with nc.Block() as block:
                    @block.vector
                    def _(dve):
                        link = chained(dve, f"chain_2{way}", c)
                        three_parts(dve, link, [us[:, :, i, :] for i in range(3)], tab[:, :, way * H2:(way + 1) * H2], rest[:, :, :])
                store([(to, us[:, :, :, :].rearrange("p b i w -> p b (i w)"))], c, f"st2{way}")

        def flow_pass(name, c, k, rows, local, W1, W2, b2, acc, first):
            FW = D + DE
            ps = Pass(name, c, k, D, gath[2], rows, local, feats=True)
            featT = ps.ring("featT", [2 * FW, GE // 2], F32, 2)
            hid = ps.ring("hid", [2 * H2, GE // 2], F32, 2)
            msg = ps.ring("msg", [P, T * D], F32, 2)
            w1 = diagonal(c, name + "w1", [(0, W1[D:2 * D + DE, :])], 2, H2, FW)
            w2 = diagonal(c, name + "w2", [(0, W2)], 2, D)
            ps.splitter(T * D)
            b2r = bias_rows(c, name + "b2r", [(0, b2)], D, 2)
            b2s = ps.sb("b2s", [1, 3, 2 * D], BF16)
            b2rest = ps.sb("b2rest", [1, 2 * D], F32)
            s_zero, s_turn, s_turned, s_hid, s_rect, s_out, s_msg, s_carry = (
                ps.sem(n) for n in ("zero", "turn", "turned", "hid", "rect", "out", "msg", "carry"))
            with nc.Block() as block:
                @block.vector
                def _(dve):
                    three_parts(dve, chained(dve, f"chain_{name}", c), [b2s[:, i, :] for i in range(3)], b2r, b2rest[:, :])
            with nc.Block() as block:
                @block.sync
                def _(sp):
                    ps.feed(sp)

                @block.gpsimd
                def _(pool):
                    ps.gather(pool)

                @block.vector
                def _(dve):
                    if first:
                        dve.memset(acc[:, :, :], 0.0).then_inc(s_zero, 1)
                        dve.wait_ge(s_zero, 1)
                    for step in group_steps(dve, NG, U, 5):
                        if at := step(0):
                            list(ps.edges_hot(dve, at))
                        if at := step(3):
                            dve.wait_ge(s_msg, at.g + 1)
                            list(ps.split(dve, at, msg[at.slot % 2][:, :]))
                        if at := step(5):
                            ps.add(dve, at, acc[:, :, k * D:(k + 1) * D], D)

                @block.scalar
                def _(act):
                    for step in group_steps(act, NG, U, 5):
                        if at := step(3):
                            if not (isinstance(at.g, int) and at.g < 2):
                                act.wait_ge(s_hid, at.g - 1)
                            act.wait_ge(s_turn, at.g + 1)
                            act.activation(featT[at.slot % 2][:, :], psum[0][0:2 * FW, 0:GE // 2], ACT.Copy).then_inc(s_turned, 1)
                        if at := step(4):
                            if not (isinstance(at.g, int) and at.g < 2):
                                act.wait_ge(s_out, at.g - 1)
                            act.wait_ge(s_hid, at.g + 1)
                            act.activation(hid[at.slot % 2][:, :], psum[2][:, 0:GE // 2], ACT.Relu).then_inc(s_rect, 1)
                        if at := step(5):
                            if not (isinstance(at.g, int) and at.g < 2):
                                act.wait_ge(ps.split_done, at.g * 4 - 4)
                            act.wait_ge(s_out, at.g + 1)
                            act.activation(msg[at.slot % 2][:, :], psum[3][:, 0:T * D], ACT.Relu).then_inc(s_msg, 1)
                        if at := step(0):
                            ps.load(act, at)

                @block.tensor
                def _(pe):
                    for step in group_steps(pe, NG, U, 4):
                        if at := step(0):
                            pe.wait_ge(ps.loaded[at.slot], ps.here(at))
                            if not (isinstance(at.g, int) and at.g == 0):
                                pe.wait_ge(s_turned, at.g)
                            pe.sem_inc(s_carry, 1)
                            for p in range(T // 2):
                                ins = pe.transpose(psum[0][0:2 * FW, p * P:(p + 1) * P],
                                                   ps.far[at.slot][:, 2 * p:2 * p + 2, :].rearrange("p j w -> p (j w)"), ident[:, :])
                            ins.then_inc(s_turn, 1)
                        if at := step(1):
                            pe.wait_ge(ps.hot, at.g + 1)
                            if not (isinstance(at.g, int) and at.g == 0):
                                pe.wait_ge(s_rect, at.g)
                            pe.wait_ge(s_turned, at.g + 1)
                            pe.sem_inc(s_carry, 1)
                            pe.matmul(psum[2][:, 0:GE // 2], w1[0:2 * FW, :], featT[at.slot % 2][:, :], start=True, stop=False,
                                      skip_group_check=True)
                            pairs = ps.ot[at.slot][:, :, :].rearrange("n p (q s) -> n s q p", s=2)
                            for half in range(2):
                                for i in range(3):
                                    ins = pe.matmul(psum[2][half * H2:(half + 1) * H2, 0:GE // 2], ps.loc[at.slot][:, i * H2:(i + 1) * H2],
                                                    pairs[:, half, :, :], start=False, stop=i == 2, skip_group_check=True)
                            ins.then_inc(s_hid, 1)
                        if at := step(2):
                            pe.wait_ge(s_rect, at.g + 1)
                            if not (isinstance(at.g, int) and at.g == 0):
                                pe.wait_ge(s_msg, at.g)
                            for p in range(T // 2):
                                to = psum[3][:, p * 2 * D:(p + 1) * 2 * D]
                                for i in range(3):
                                    pe.matmul(to, onesb[0:1, :], b2s[:, i, :], start=i == 0, stop=False)
                                ins = pe.matmul(to, hid[at.slot % 2][:, p * P:(p + 1) * P], w2[:, :], start=False, stop=True)
                            ins.then_inc(s_out, 1)
                        if at := step(4):
                            pe.wait_ge(ps.split_done, ps.split_at(at))
                            ps.segment_sum(pe, at, lambda j, i: ps.part[at.slot % 2][:, i, j * D:(j + 1) * D], D, 3)

        with Scope() as c:
            flows = sb("flows", [P, NBP, 2 * D], F32, c)
            with Scope() as c2:
                flow_pass("l2f", c2, 0, rows[2], locl[2], W1f, W2f, b2f, flows, True)
            with Scope() as c2:
                flow_pass("l2b", c2, 1, rows[4], locl[4], W1b, W2b, b2b, flows, False)
            w1n = diagonal(c, "w1n", [(0, W1n)], 2, H2)
            w2n = diagonal(c, "w2n", [(0, W2n)], 2, D)
            b1c = sb("b1c", [P, 1], F32, c)
            s_b1 = sem("s_b1", c)
            with nc.Block() as block:
                @block.sync
                def _(sp):
                    for r in range(2):
                        sp.dma_start(b1c[r * H2:(r + 1) * H2, :], b1n.unsqueeze(1)).then_inc(s_b1, 16)
                    sp.wait_ge(s_b1, 32)
            bias = bias_rows(c, "bias2n", [(0, b2n)], D, 2)
            node_matmul("n2n", c, NBP // 2, lambda dve, i, to: dve.tensor_copy(to[:, :].rearrange("p (r f) -> p r f", r=2), flows[:, ds(i * 2, 2), :]),
                        w2n[:, :], bias, put0, hidden=(w1n, b1c))

        with Scope() as c:
            normalise(c)
            tab = sb("tab3", [P, NBP, 2 * HEADS], F32, c)
            w = sb("w3a", [P, 4, 4 * HEADS * 2 // 4], F32, c)
            w3r = sb("w3r", [P, HEADS, D], F32, c)
            fcr = sb("fcr", [P, 2, D], F32, c)
            prod3 = sb("prod3", [P, HEADS, D], F32, c)
            col = sb("col3", [P, 2, HEADS], F32, c)
            bias = sb("bias3a", [1, 4, 2, HEADS], F32, c)
            fcb = sb("fcb", [1, 1], F32, c)
            s_w3 = sem("s_w3", c)
            with nc.Block() as block:
                @block.sync
                def _(sp):
                    for r in range(4):
                        sp.dma_start(w3r[r * D:(r + 1) * D, :, :], w3.rearrange("h f o -> f h o")).then_inc(s_w3, 16)
                    sp.dma_start(fcr[:, :, :].rearrange("p a o -> p (a o)"), fc_w[0:1, :].to_broadcast([P, 2 * D])).then_inc(s_w3, 16)
                    sp.dma_start(fcb[:, :], fc_b.unsqueeze(0)).then_inc(s_w3, 16)

                @block.vector
                def _(dve):
                    link = chained(dve, "chain_3", c)
                    link(dve.memset(w[:, :, :], 0.0))
                    link(dve.memset(bias[:, :, :, :], 0.0))
                    dve.wait_ge(s_w3, 96)
                    for a in range(2):
                        link(dve.tensor_tensor(prod3[:, :, :], w3r[:, :, :], fcr[:, a:a + 1, :].to_broadcast([P, HEADS, D]), ALU.mult))
                        link(dve.tensor_reduce(col[:, a, :], prod3[:, :, :], X, ALU.add))
                    for r in range(4):
                        link(dve.tensor_copy(w[r * D:(r + 1) * D, r, :], col[r * D:(r + 1) * D, :, :].rearrange("p a h -> p (a h)")))
                    link(dve.tensor_scalar(bias[:, :, 0, :], bias[:, :, 0, :], fcb[0:1, 0:1], None, ALU.add))
            node_matmul("n3", c, NBP // 4, lambda dve, i, to: dve.tensor_copy(to[:, :].rearrange("p (r f) -> p r f", r=4), Hs[:, ds(i * 4, 4), :]),
                        w[:, :, :].rearrange("p r w -> p (r w)"), bias[:, :, :, :].rearrange("a r k h -> a (r k h)"),
                        lambda dve, i, value: dve.tensor_copy(tab[:, ds(i * 4, 4), :].rearrange("p r w -> p (r w)"), value))
            near3 = sb("near3", [P, NBP, 3, HEADS], BF16, c)
            rest = sb("rest3", [P, NBP, HEADS], F32, c)
            far3 = sb("far3", [P, NBP, D + HEADS], F32, c)
            with nc.Block() as block:
                @block.vector
                def _(dve):
                    link = chained(dve, "chain_3b", c)
                    three_parts(dve, link, [near3[:, :, i, :] for i in range(3)], tab[:, :, 0:HEADS], rest[:, :, :])
                    dve.tensor_copy(far3[:, :, 0:D], Hs[:, :, :])
                    dve.tensor_copy(far3[:, :, D:D + HEADS], tab[:, :, HEADS:2 * HEADS])
            store([(locl[3], near3[:, :, :, :].rearrange("p b i w -> p b (i w)")), (gath[3], far3[:, :, :])], c, "st3")

        with Scope() as c:
            HW = D + 1
            acc = sb("acc3", [P, NBP, HEADS * HW], F32, c)
            best = sb("best3", [P, NBP, HEADS], F32, c)
            with Scope() as c2:
                raw = [sb(f"raw{u}", [P, T, HEADS], F32, c2) for u in range(2)]

                def score3(dve, at, far, sc, s_tmp, s_sc):
                    r = raw[at.slot % 2]
                    dve.tensor_tensor(r[:, :, :], psum[0][:, 0:T * HEADS].rearrange("p (j h) -> p j h", j=T), far[at.slot][:, :, D:D + HEADS],
                                      ALU.add).then_inc(s_tmp, 1)
                    yield
                    dve.wait_ge(s_tmp, at.g + 1)
                    dve.scalar_tensor_tensor(sc[:, :, :], r[:, :, :], 0.2, r[:, :, :], ALU.mult, ALU.max).then_inc(s_sc, 1)
                    yield

                def spread3(dve, far, val):
                    return dve.tensor_tensor(val[:, :, :, 0:D], far[:, :, 0:D].unsqueeze(2).to_broadcast([P, T, HEADS, D]),
                                             val[:, :, :, D:D + 1].to_broadcast([P, T, HEADS, D]), ALU.mult)
                softmax_pass("l3", c2, 1, D + HEADS, gath[3], rows[3], locl[3], HW, acc, best, near_part(HEADS), score3, spread3, 1)
            den = sb("den3", [P, NBP, HEADS], F32, c)
            w = sb("w3b", [P, D], F32, c)
            s_w3b = sem("s_w3b", c)
            with nc.Block() as block:
                @block.sync
                def _(sp):
                    sp.dma_start(w[:, :], w3.rearrange("h f o -> (h f) o")).then_inc(s_w3b, 16)

                @block.vector
                def _(dve):
                    link = chained(dve, "chain_3c", c)
                    a4 = acc[:, :, :].rearrange("p b (h w) -> p b h w", h=HEADS)
                    link(dve.tensor_scalar(den[:, :, :], a4[:, :, :, D], 1e-30, None, ALU.max))
                    link(dve.reciprocal(den[:, :, :], den[:, :, :]))
                    dve.tensor_tensor(a4[:, :, :, 0:D], a4[:, :, :, 0:D], den[:, :, :].unsqueeze(3).to_broadcast([P, NBP, HEADS, D]), ALU.mult)
                    dve.wait_ge(s_w3b, 16)
                    dve.tensor_scalar(w[:, :], w[:, :], 1.0 / HEADS, None, ALU.mult)
            bias = bias_rows(c, "bias3", [(0, bias3)], D, 1)
            node_matmul("n3b", c, NBP,
                        lambda dve, i, to: dve.tensor_copy(to[:, :].rearrange("p (h f) -> p h f", h=HEADS),
                                                           acc[:, ds(i, 1), :].rearrange("p a (h w) -> p (a h) w", h=HEADS)[:, :, 0:D]),
                        w[:, :], bias, add_rows(1))
            s_res = sem("s_res", c)
            with nc.Block() as block:
                @block.sync
                def _(sp):
                    sp.dma_start(out[0:FULL * P, :].rearrange("(b p) f -> p b f", p=P), Xs[:, 0:FULL, :]).then_inc(s_res, 16)
                    sp.dma_start(out[FULL * P:N, :], Xs[0:N - FULL * P, FULL, :]).then_inc(s_res, 16)
                    sp.wait_ge(s_res, 32)


_INS = ['x', 'src', 'dst', 'edge_attr_16', 'L0_gnn_W', 'L0_gnn_b', 'L1_gnn_Wq', 'L1_gnn_Wk', 'L1_gnn_Wv', 'L1_gnn_Wo',
        'L2_gnn_W1f', 'L2_gnn_b1f', 'L2_gnn_W2f', 'L2_gnn_b2f', 'L2_gnn_W1b', 'L2_gnn_b1b', 'L2_gnn_W2b', 'L2_gnn_b2b',
        'L2_gnn_W1n', 'L2_gnn_b1n', 'L2_gnn_W2n', 'L2_gnn_b2n', 'L3_gnn_w', 'L3_gnn_fc_w', 'L3_gnn_fc_b', 'L3_gnn_bias']


def kernel(**inputs):
    import numpy as _np
    import concourse.bacc as _bacc
    from concourse import mybir as _mybir
    from concourse.bass_utils import run_bass_kernel_spmd as _run

    nc = _bacc.Bacc("TRN2", target_bir_lowering=False, num_devices=1)
    arrays, args = {}, []
    for name in _INS:
        a = _np.ascontiguousarray(inputs[name])
        arrays[f"in_{name}_dram"] = a
        args.append(nc.dram_tensor(f"in_{name}_dram", a.shape, _mybir.dt.from_np(a.dtype), kind="ExternalInput").ap())
    args.append(nc.dram_tensor("out_dram", (N, D), _mybir.dt.float32, kind="ExternalOutput").ap())
    gnn_kernel(nc, *args)
    r = _run(nc, [arrays], core_ids=[0])
    return r.results[0]["out_dram"]
```
